# Optimizing a Trainium2 kernel written in Bass

```python
import numpy as np
import jax
import jax.numpy as jnp

def _softmax(x, axis=-1):
    return jax.nn.softmax(x, axis=axis)

def _gelu(x):
    return jax.nn.gelu(x, approximate=True)

def _silu(x):
    return jax.nn.silu(x)

def _sigmoid(x):
    return jax.nn.sigmoid(x)

def _layernorm(x, axis=-1, eps=1e-05):
    m = jnp.mean(x, axis=axis, keepdims=True)
    v = jnp.var(x, axis=axis, keepdims=True)
    return (x - m) / jnp.sqrt(v + eps)

def _scatter_add(tgt, idx, src, axis=0):
    return tgt.at[idx].add(src)

def _segment_sum(src, seg, n):
    return jax.ops.segment_sum(src, seg, n)
kernel_name = 'mk_xattn_seq_d4_seqx_r8_3b883f'

def setup_inputs(seed: int=0):
    np.random.seed(seed)
    _w = jnp.asarray

    def _rec_inputs():
        import jax
        import jax.numpy as jnp
        _rk = jax.random.key(seed)
        x = 7.22e-05 + 1 * jax.random.normal(jax.random.fold_in(_rk, 1), (8, 128, 256), jnp.float32)
        _lenS = 128 - jax.random.randint(jax.random.fold_in(_rk, 7), (8,), 0, max(1, 128 // 4) + 1, jnp.int32)
        _lenS2 = 128 - jax.random.randint(jax.random.fold_in(_rk, 8), (8,), 0, max(1, 128 // 4) + 1, jnp.int32)
        _ctx_1024P = jax.random.normal(jax.random.fold_in(_rk, 11), (8, 16, 128), jnp.float32)
        _ctx_1024c = jax.random.dirichlet(jax.random.fold_in(_rk, 511), 0.3 * jnp.ones((16,), jnp.float32), (8, 128))
        _ctx_1024t = jnp.einsum('bsk,bkd->bsd', _ctx_1024c, _ctx_1024P)
        _ctx_1024t = _ctx_1024t * jax.lax.rsqrt(jnp.mean(jnp.square(_ctx_1024t)) + 1e-12) * 0.953939
        ctx_1024 = -0.000514642 + 1.00011 * (_ctx_1024t + 0.3 * jax.random.normal(jax.random.fold_in(_rk, 611), (8, 128, 128), jnp.float32))
        pos_1xS = jnp.broadcast_to(jnp.arange(128, dtype=jnp.int32), (1, 128))
        _validS = jnp.arange(128)[None, :] < _lenS[:, None]
        _validS2 = jnp.arange(128)[None, :] < _lenS2[:, None]
        _causal = jnp.tril(jnp.ones((128, 128), dtype=bool))
        mask_BxS_ik0 = jnp.where(jnp.broadcast_to(_validS[:, :], (8, 128)), 0, 1).astype(jnp.int32)
        mask_BxS2_bk0 = jnp.logical_not(jnp.broadcast_to(_validS2[:, :], (8, 128)))
        return (x, ctx_1024, pos_1xS, mask_BxS_ik0, mask_BxS2_bk0)
    x, ctx_1024, pos_1xS, mask_BxS_ik0, mask_BxS2_bk0 = _rec_inputs()

    def _L0_xattn_setup():
        import jax, jax.numpy as jnp
        import numpy as np
        H = 256
        NH = 16
        HD = H // NH
        CH = 128
        CC = 128
        CHD = CC // NH
        I = 688
        B = 2
        L = 256
        LE = 128
        EPS = 1e-06

        def rms_norm(x, w):
            xf = x.astype(jnp.float32)
            var = jnp.mean(xf * xf, axis=-1, keepdims=True)
            return (w * (xf * jax.lax.rsqrt(var + EPS))).astype(x.dtype)

        def expert_mask(tt):
            vm = jnp.zeros(tt.shape, dtype=bool)
            vm = vm.at[:, :-1].set((tt[:, :-1] == 1) & (tt[:, 1:] == 1))
            return vm

        def rotate_half(x):
            d = x.shape[-1] // 2
            return jnp.concatenate([-x[..., d:], x[..., :d]], axis=-1)

        def apply_rotary(q, k, position_ids, seq_len):
            inv = 1.0 / 10000.0 ** (jnp.arange(0, HD, 2, dtype=jnp.float32) / HD)
            t = jnp.arange(seq_len, dtype=jnp.float32)
            freqs = jnp.outer(t, inv)
            emb = jnp.concatenate([freqs, freqs], axis=-1)
            cos = jnp.cos(emb)[position_ids][:, None].astype(q.dtype)
            sin = jnp.sin(emb)[position_ids][:, None].astype(q.dtype)
            return (q * cos + rotate_half(q) * sin, k * cos + rotate_half(k) * sin)

        def sdpa(q, k, v, causal):
            scale = 1.0 / np.sqrt(q.shape[-1])
            scores = jnp.einsum('bhqd,bhkd->bhqk', q * scale, k)
            if causal:
                mask = jnp.tril(jnp.ones((q.shape[-2], k.shape[-2]), dtype=bool))
                scores = jnp.where(mask, scores, jnp.finfo(jnp.float32).min)
            p = jax.nn.softmax(scores.astype(jnp.float32), axis=-1).astype(q.dtype)
            return jnp.einsum('bhqk,bhkd->bhqd', p, v)

        def heads(x, nh, hd):
            b, l, _ = x.shape
            return x.reshape(b, l, nh, hd).transpose(0, 2, 1, 3)
        key = jax.random.key(seed)
        ks = jax.random.split(key, 20)
        s = 0.02
        f32 = jnp.float32
        return {'hidden_states': jax.random.normal(ks[0], (B, L, H), f32), 'encoder_outputs': jax.random.normal(ks[1], (B, LE, CH), f32), 'token_type_ids': jax.random.randint(ks[2], (B, L), 0, 2, jnp.int32), 'position_ids': jnp.arange(L, dtype=jnp.int32)[None, :], 'ln_in_w': jnp.ones((H,), f32), 'ln_post_attn_w': jnp.ones((H,), f32), 'ln_post_cross_w': jnp.ones((H,), f32), 'v_qkv': jax.random.normal(ks[3], (H, 3 * H), f32) * s, 'l_qkv': jax.random.normal(ks[4], (H, 3 * H), f32) * s, 'v_dense': jax.random.normal(ks[5], (H, H), f32) * s, 'l_dense': jax.random.normal(ks[6], (H, H), f32) * s, 'cq_w': jax.random.normal(ks[7], (H, CC), f32) * s, 'ckv_w': jax.random.normal(ks[8], (CH, 2 * CC), f32) * s, 'cdense_w': jax.random.normal(ks[9], (CC, H), f32) * s, 'v_gate': jax.random.normal(ks[10], (H, I), f32) * s, 'v_up': jax.random.normal(ks[11], (H, I), f32) * s, 'v_down': jax.random.normal(ks[12], (I, H), f32) * s, 'l_gate': jax.random.normal(ks[13], (H, I), f32) * s, 'l_up': jax.random.normal(ks[14], (H, I), f32) * s, 'l_down': jax.random.normal(ks[15], (I, H), f32) * s}
    _L0_xattn_all = _L0_xattn_setup()
    _L0_xattn_in = {k: v for k, v in _L0_xattn_all.items() if k in ('ln_in_w', 'ln_post_attn_w', 'ln_post_cross_w', 'v_qkv', 'l_qkv', 'v_dense', 'l_dense', 'cq_w', 'ckv_w', 'cdense_w', 'v_gate', 'v_up', 'v_down', 'l_gate', 'l_up', 'l_down')}
    del _L0_xattn_all

    def _L1_xattn_setup():
        import jax, jax.numpy as jnp
        import numpy as np
        EPS = 1e-06

        def _rmsnorm(x, w):
            var = jnp.mean(jnp.square(x), axis=-1, keepdims=True)
            return x * jax.lax.rsqrt(var + EPS) * w
        key = jax.random.key(seed)
        ks = jax.random.split(key, 6)
        B, N, M = (4, 512, 256)
        d_model, memory_dim = (256, 128)
        hidden_states = jax.random.normal(ks[0], (B, N, d_model), dtype=jnp.float32)
        memory = jax.random.normal(ks[1], (B, M, memory_dim), dtype=jnp.float32)
        W_mem = jax.random.normal(ks[2], (d_model, memory_dim), dtype=jnp.float32) / np.sqrt(memory_dim)
        W_gate = jax.random.normal(ks[3], (d_model, 2 * d_model), dtype=jnp.float32) / np.sqrt(2 * d_model)
        b_gate = jax.random.normal(ks[4], (d_model,), dtype=jnp.float32) * 0.01
        norm_w = jnp.ones((d_model,), dtype=jnp.float32)
        return {'hidden_states': hidden_states, 'memory': memory, 'W_mem': W_mem, 'W_gate': W_gate, 'b_gate': b_gate, 'norm_w': norm_w}
    _L1_xattn_all = _L1_xattn_setup()
    _L1_xattn_in = {k: v for k, v in _L1_xattn_all.items() if k in ('W_mem', 'W_gate', 'b_gate', 'norm_w')}
    del _L1_xattn_all

    def _L2_xattn_setup():
        import jax, jax.numpy as jnp
        import numpy as np
        DIM = 256
        DIM_MEDIA = 128
        HEADS = 16
        DIM_HEAD = 64
        INNER = HEADS * DIM_HEAD
        FF_INNER = 4 * DIM
        B, N_TOK, N_LAT = (4, 256, 64)
        EPS = 1e-05

        def layernorm(x, g, b):
            mu = jnp.mean(x, axis=-1, keepdims=True)
            var = jnp.var(x, axis=-1, keepdims=True)
            return (x - mu) * jax.lax.rsqrt(var + EPS) * g + b
        key = jax.random.key(seed)
        ks = jax.random.split(key, 12)
        x = jax.random.normal(ks[0], (B, N_TOK, DIM), dtype=jnp.float32)
        media = jax.random.normal(ks[1], (B, N_LAT, DIM_MEDIA), dtype=jnp.float32)
        media_mask = jax.random.randint(ks[2], (B, N_LAT), 0, 2).astype(bool)
        media_mask = media_mask.at[:, 0].set(True)
        s = lambda d: 1.0 / np.sqrt(d)
        Wq = jax.random.normal(ks[3], (DIM, INNER), dtype=jnp.float32) * s(DIM)
        Wkv = jax.random.normal(ks[4], (DIM_MEDIA, 2 * INNER), dtype=jnp.float32) * s(DIM_MEDIA)
        Wo = jax.random.normal(ks[5], (INNER, DIM), dtype=jnp.float32) * s(INNER)
        W1 = jax.random.normal(ks[6], (DIM, FF_INNER), dtype=jnp.float32) * s(DIM)
        W2 = jax.random.normal(ks[7], (FF_INNER, DIM), dtype=jnp.float32) * s(FF_INNER)
        return {'x': x, 'media': media, 'media_mask': media_mask, 'ln_q_g': jnp.ones((DIM,), jnp.float32), 'ln_q_b': jnp.zeros((DIM,), jnp.float32), 'Wq': Wq, 'Wkv': Wkv, 'Wo': Wo, 'attn_gate': jax.random.normal(ks[8], (1,), jnp.float32) * 0.5, 'ln_ff_g': jnp.ones((DIM,), jnp.float32), 'ln_ff_b': jnp.zeros((DIM,), jnp.float32), 'W1': W1, 'W2': W2, 'ff_gate': jax.random.normal(ks[9], (1,), jnp.float32) * 0.5}
    _L2_xattn_all = _L2_xattn_setup()
    _L2_xattn_in = {k: v for k, v in _L2_xattn_all.items() if k in ('ln_q_g', 'ln_q_b', 'Wq', 'Wkv', 'Wo', 'attn_gate', 'ln_ff_g', 'ln_ff_b', 'W1', 'W2', 'ff_gate')}
    del _L2_xattn_all

    def _L3_xattn_setup():
        import jax, jax.numpy as jnp
        import numpy as np
        EPS = 1e-06

        def _rmsnorm(x, w):
            var = jnp.mean(jnp.square(x), axis=-1, keepdims=True)
            return x * jax.lax.rsqrt(var + EPS) * w
        key = jax.random.key(seed)
        ks = jax.random.split(key, 6)
        B, N, M = (4, 512, 256)
        d_model, memory_dim = (256, 128)
        hidden_states = jax.random.normal(ks[0], (B, N, d_model), dtype=jnp.float32)
        memory = jax.random.normal(ks[1], (B, M, memory_dim), dtype=jnp.float32)
        W_mem = jax.random.normal(ks[2], (d_model, memory_dim), dtype=jnp.float32) / np.sqrt(memory_dim)
        W_gate = jax.random.normal(ks[3], (d_model, 2 * d_model), dtype=jnp.float32) / np.sqrt(2 * d_model)
        b_gate = jax.random.normal(ks[4], (d_model,), dtype=jnp.float32) * 0.01
        norm_w = jnp.ones((d_model,), dtype=jnp.float32)
        return {'hidden_states': hidden_states, 'memory': memory, 'W_mem': W_mem, 'W_gate': W_gate, 'b_gate': b_gate, 'norm_w': norm_w}
    _L3_xattn_all = _L3_xattn_setup()
    _L3_xattn_in = {k: v for k, v in _L3_xattn_all.items() if k in ('W_mem', 'W_gate', 'b_gate', 'norm_w')}
    del _L3_xattn_all
    return {'x': x, 'ctx_1024': ctx_1024, 'pos_1xS': pos_1xS, 'mask_BxS_ik0': mask_BxS_ik0, 'mask_BxS2_bk0': mask_BxS2_bk0, 'L0_xattn_ln_in_w': _L0_xattn_in['ln_in_w'], 'L0_xattn_ln_post_attn_w': _L0_xattn_in['ln_post_attn_w'], 'L0_xattn_ln_post_cross_w': _L0_xattn_in['ln_post_cross_w'], 'L0_xattn_v_qkv': _L0_xattn_in['v_qkv'], 'L0_xattn_l_qkv': _L0_xattn_in['l_qkv'], 'L0_xattn_v_dense': _L0_xattn_in['v_dense'], 'L0_xattn_l_dense': _L0_xattn_in['l_dense'], 'L0_xattn_cq_w': _L0_xattn_in['cq_w'], 'L0_xattn_ckv_w': _L0_xattn_in['ckv_w'], 'L0_xattn_cdense_w': _L0_xattn_in['cdense_w'], 'L0_xattn_v_gate': _L0_xattn_in['v_gate'], 'L0_xattn_v_up': _L0_xattn_in['v_up'], 'L0_xattn_v_down': _L0_xattn_in['v_down'], 'L0_xattn_l_gate': _L0_xattn_in['l_gate'], 'L0_xattn_l_up': _L0_xattn_in['l_up'], 'L0_xattn_l_down': _L0_xattn_in['l_down'], 'L1_xattn_W_mem': _L1_xattn_in['W_mem'], 'L1_xattn_W_gate': _L1_xattn_in['W_gate'], 'L1_xattn_b_gate': _L1_xattn_in['b_gate'], 'L1_xattn_norm_w': _L1_xattn_in['norm_w'], 'L2_xattn_ln_q_g': _L2_xattn_in['ln_q_g'], 'L2_xattn_ln_q_b': _L2_xattn_in['ln_q_b'], 'L2_xattn_Wq': _L2_xattn_in['Wq'], 'L2_xattn_Wkv': _L2_xattn_in['Wkv'], 'L2_xattn_Wo': _L2_xattn_in['Wo'], 'L2_xattn_attn_gate': _L2_xattn_in['attn_gate'], 'L2_xattn_ln_ff_g': _L2_xattn_in['ln_ff_g'], 'L2_xattn_ln_ff_b': _L2_xattn_in['ln_ff_b'], 'L2_xattn_W1': _L2_xattn_in['W1'], 'L2_xattn_W2': _L2_xattn_in['W2'], 'L2_xattn_ff_gate': _L2_xattn_in['ff_gate'], 'L3_xattn_W_mem': _L3_xattn_in['W_mem'], 'L3_xattn_W_gate': _L3_xattn_in['W_gate'], 'L3_xattn_b_gate': _L3_xattn_in['b_gate'], 'L3_xattn_norm_w': _L3_xattn_in['norm_w']}

def reference(x, ctx_1024, pos_1xS, mask_BxS_ik0, mask_BxS2_bk0, L0_xattn_ln_in_w, L0_xattn_ln_post_attn_w, L0_xattn_ln_post_cross_w, L0_xattn_v_qkv, L0_xattn_l_qkv, L0_xattn_v_dense, L0_xattn_l_dense, L0_xattn_cq_w, L0_xattn_ckv_w, L0_xattn_cdense_w, L0_xattn_v_gate, L0_xattn_v_up, L0_xattn_v_down, L0_xattn_l_gate, L0_xattn_l_up, L0_xattn_l_down, L1_xattn_W_mem, L1_xattn_W_gate, L1_xattn_b_gate, L1_xattn_norm_w, L2_xattn_ln_q_g, L2_xattn_ln_q_b, L2_xattn_Wq, L2_xattn_Wkv, L2_xattn_Wo, L2_xattn_attn_gate, L2_xattn_ln_ff_g, L2_xattn_ln_ff_b, L2_xattn_W1, L2_xattn_W2, L2_xattn_ff_gate, L3_xattn_W_mem, L3_xattn_W_gate, L3_xattn_b_gate, L3_xattn_norm_w):
    import jax
    import jax.numpy as jnp

    def _L0_xattn_ref(hidden_states, encoder_outputs, token_type_ids, position_ids, ln_in_w, ln_post_attn_w, ln_post_cross_w, v_qkv, l_qkv, v_dense, l_dense, cq_w, ckv_w, cdense_w, v_gate, v_up, v_down, l_gate, l_up, l_down):
        import jax, jax.numpy as jnp
        import numpy as np
        H = 256
        NH = 16
        HD = H // NH
        CH = 128
        CC = 128
        CHD = CC // NH
        I = 688
        B = 2
        L = 256
        LE = 128
        EPS = 1e-06

        def rms_norm(x, w):
            xf = x.astype(jnp.float32)
            var = jnp.mean(xf * xf, axis=-1, keepdims=True)
            return (w * (xf * jax.lax.rsqrt(var + EPS))).astype(x.dtype)

        def expert_mask(tt):
            vm = jnp.zeros(tt.shape, dtype=bool)
            vm = vm.at[:, :-1].set((tt[:, :-1] == 1) & (tt[:, 1:] == 1))
            return vm

        def rotate_half(x):
            d = x.shape[-1] // 2
            return jnp.concatenate([-x[..., d:], x[..., :d]], axis=-1)

        def apply_rotary(q, k, position_ids, seq_len):
            inv = 1.0 / 10000.0 ** (jnp.arange(0, HD, 2, dtype=jnp.float32) / HD)
            t = jnp.arange(seq_len, dtype=jnp.float32)
            freqs = jnp.outer(t, inv)
            emb = jnp.concatenate([freqs, freqs], axis=-1)
            cos = jnp.cos(emb)[position_ids][:, None].astype(q.dtype)
            sin = jnp.sin(emb)[position_ids][:, None].astype(q.dtype)
            return (q * cos + rotate_half(q) * sin, k * cos + rotate_half(k) * sin)

        def sdpa(q, k, v, causal):
            scale = 1.0 / np.sqrt(q.shape[-1])
            scores = jnp.einsum('bhqd,bhkd->bhqk', q * scale, k)
            if causal:
                mask = jnp.tril(jnp.ones((q.shape[-2], k.shape[-2]), dtype=bool))
                scores = jnp.where(mask, scores, jnp.finfo(jnp.float32).min)
            p = jax.nn.softmax(scores.astype(jnp.float32), axis=-1).astype(q.dtype)
            return jnp.einsum('bhqk,bhkd->bhqd', p, v)

        def heads(x, nh, hd):
            b, l, _ = x.shape
            return x.reshape(b, l, nh, hd).transpose(0, 2, 1, 3)
        b, l, _ = hidden_states.shape
        vm = expert_mask(token_type_ids)[..., None]
        residual = hidden_states
        x = rms_norm(hidden_states, ln_in_w)
        mixed = jnp.where(vm, x @ v_qkv, x @ l_qkv)
        q, k, v = jnp.split(mixed, 3, axis=-1)
        q, k, v = (heads(q, NH, HD), heads(k, NH, HD), heads(v, NH, HD))
        q, k = apply_rotary(q, k, position_ids, l)
        ctx = sdpa(q, k, v, causal=True)
        ctx = ctx.transpose(0, 2, 1, 3).reshape(b, l, H)
        attn_out = jnp.where(vm, ctx @ v_dense, ctx @ l_dense)
        hidden_states = residual + attn_out
        ci = rms_norm(hidden_states, ln_post_cross_w)
        cq = heads(ci @ cq_w, NH, CHD)
        ckv = encoder_outputs @ ckv_w
        ck, cv = jnp.split(ckv, 2, axis=-1)
        ck, cv = (heads(ck, NH, CHD), heads(cv, NH, CHD))
        cctx = sdpa(cq, ck, cv, causal=False)
        cctx = cctx.transpose(0, 2, 1, 3).reshape(b, l, CC)
        hidden_states = hidden_states + cctx @ cdense_w
        mi = rms_norm(hidden_states, ln_post_attn_w)
        v_out = jax.nn.silu(mi @ v_gate) * (mi @ v_up) @ v_down
        l_out = jax.nn.silu(mi @ l_gate) * (mi @ l_up) @ l_down
        hidden_states = hidden_states + jnp.where(vm, v_out, l_out)
        return hidden_states

    def _L1_xattn_ref(hidden_states, memory, W_mem, W_gate, b_gate, norm_w):
        import jax, jax.numpy as jnp
        import numpy as np
        EPS = 1e-06

        def _rmsnorm(x, w):
            var = jnp.mean(jnp.square(x), axis=-1, keepdims=True)
            return x * jax.lax.rsqrt(var + EPS) * w
        D = hidden_states.shape[-1]
        memory_proj = jnp.einsum('bme,de->bmd', memory, W_mem)
        scores = jnp.einsum('bnd,bmd->bnm', hidden_states, memory_proj) / jnp.sqrt(jnp.float32(D))
        attn = jax.nn.softmax(scores, axis=-1)
        memory_context = jnp.einsum('bnm,bmd->bnd', attn, memory_proj)
        gate_input = jnp.concatenate([hidden_states, memory_context], axis=-1)
        gate = jax.nn.sigmoid(jnp.einsum('bnf,df->bnd', gate_input, W_gate) + b_gate)
        fused = hidden_states + gate * memory_context
        return _rmsnorm(fused, norm_w)

    def _L2_xattn_ref(x, media, media_mask, ln_q_g, ln_q_b, Wq, Wkv, Wo, attn_gate, ln_ff_g, ln_ff_b, W1, W2, ff_gate):
        import jax, jax.numpy as jnp
        import numpy as np
        DIM = 256
        DIM_MEDIA = 128
        HEADS = 16
        DIM_HEAD = 64
        INNER = HEADS * DIM_HEAD
        FF_INNER = 4 * DIM
        B, N_TOK, N_LAT = (4, 256, 64)
        EPS = 1e-05

        def layernorm(x, g, b):
            mu = jnp.mean(x, axis=-1, keepdims=True)
            var = jnp.var(x, axis=-1, keepdims=True)
            return (x - mu) * jax.lax.rsqrt(var + EPS) * g + b
        scale = DIM_HEAD ** (-0.5)
        qn = layernorm(x, ln_q_g, ln_q_b)
        q = qn @ Wq * scale
        kv = media @ Wkv
        k, v = jnp.split(kv, 2, axis=-1)
        split_heads = lambda t: t.reshape(t.shape[0], t.shape[1], HEADS, DIM_HEAD).transpose(0, 2, 1, 3)
        q, k, v = (split_heads(q), split_heads(k), split_heads(v))
        sim = jnp.einsum('bhid,bhjd->bhij', q, k)
        neg_inf = jnp.finfo(sim.dtype).min
        sim = jnp.where(media_mask[:, None, None, :], sim, neg_inf)
        attn = jax.nn.softmax(sim, axis=-1)
        out = jnp.einsum('bhij,bhjd->bhid', attn, v)
        out = out.transpose(0, 2, 1, 3).reshape(x.shape[0], x.shape[1], INNER)
        attn_out = out @ Wo
        x = x + jnp.tanh(attn_gate) * attn_out
        h = layernorm(x, ln_ff_g, ln_ff_b)
        h = jax.nn.gelu(h @ W1, approximate=False) @ W2
        x = x + jnp.tanh(ff_gate) * h
        return x

    def _L3_xattn_ref(hidden_states, memory, W_mem, W_gate, b_gate, norm_w):
        import jax, jax.numpy as jnp
        import numpy as np
        EPS = 1e-06

        def _rmsnorm(x, w):
            var = jnp.mean(jnp.square(x), axis=-1, keepdims=True)
            return x * jax.lax.rsqrt(var + EPS) * w
        D = hidden_states.shape[-1]
        memory_proj = jnp.einsum('bme,de->bmd', memory, W_mem)
        scores = jnp.einsum('bnd,bmd->bnm', hidden_states, memory_proj) / jnp.sqrt(jnp.float32(D))
        attn = jax.nn.softmax(scores, axis=-1)
        memory_context = jnp.einsum('bnm,bmd->bnd', attn, memory_proj)
        gate_input = jnp.concatenate([hidden_states, memory_context], axis=-1)
        gate = jax.nn.sigmoid(jnp.einsum('bnf,df->bnd', gate_input, W_gate) + b_gate)
        fused = hidden_states + gate * memory_context
        return _rmsnorm(fused, norm_w)
    x = _L0_xattn_ref(x, ctx_1024, mask_BxS_ik0, pos_1xS, L0_xattn_ln_in_w, L0_xattn_ln_post_attn_w, L0_xattn_ln_post_cross_w, L0_xattn_v_qkv, L0_xattn_l_qkv, L0_xattn_v_dense, L0_xattn_l_dense, L0_xattn_cq_w, L0_xattn_ckv_w, L0_xattn_cdense_w, L0_xattn_v_gate, L0_xattn_v_up, L0_xattn_v_down, L0_xattn_l_gate, L0_xattn_l_up, L0_xattn_l_down)
    x = _L1_xattn_ref(x, ctx_1024, L1_xattn_W_mem, L1_xattn_W_gate, L1_xattn_b_gate, L1_xattn_norm_w)
    x = _L2_xattn_ref(x, ctx_1024, mask_BxS2_bk0, L2_xattn_ln_q_g, L2_xattn_ln_q_b, L2_xattn_Wq, L2_xattn_Wkv, L2_xattn_Wo, L2_xattn_attn_gate, L2_xattn_ln_ff_g, L2_xattn_ln_ff_b, L2_xattn_W1, L2_xattn_W2, L2_xattn_ff_gate)
    x = _L3_xattn_ref(x, ctx_1024, L3_xattn_W_mem, L3_xattn_W_gate, L3_xattn_b_gate, L3_xattn_norm_w)
    return x

_drawn_inputs = setup_inputs


def setup_inputs(seed=0):
    import zlib

    import numpy as np

    out = dict(_drawn_inputs(seed))
    spreads = {'L0_xattn_ln_in_w': (1.0, 0.6),
     'L0_xattn_ln_post_attn_w': (1.0, 0.6),
     'L0_xattn_ln_post_cross_w': (1.0, 0.6),
     'L1_xattn_norm_w': (1.0, 0.2),
     'L2_xattn_ln_q_g': (1.0, 0.6),
     'L2_xattn_ln_q_b': (0.0, 0.8),
     'L2_xattn_ln_ff_g': (1.0, 0.6),
     'L2_xattn_ln_ff_b': (0.0, 0.8),
     'L3_xattn_norm_w': (1.0, 0.2)}
    factors = {'L0_xattn_v_qkv': 8.0,
     'L0_xattn_l_qkv': 2.937,
     'L0_xattn_v_dense': 8.0,
     'L0_xattn_l_dense': 2.982,
     'L0_xattn_cq_w': 64.0,
     'L0_xattn_v_gate': 6.941,
     'L0_xattn_v_up': 6.907,
     'L0_xattn_v_down': 7.074,
     'L1_xattn_b_gate': 63.893,
     'L2_xattn_W1': 3.103,
     'L2_xattn_W2': 2.797,
     'L3_xattn_b_gate': 48.617}
    for name, (base, spread) in spreads.items():
        noise = np.random.default_rng([zlib.crc32(name.encode()), seed]).standard_normal(out[name].shape)
        drawn = base * np.exp(spread * noise) if base else spread * noise
        out[name] = jnp.asarray(drawn.astype(out[name].dtype))
    for name, factor in factors.items():
        out[name] = (out[name] * factor).astype(out[name].dtype)
    return out
```

```python
from contextlib import ExitStack

import concourse.bass as bass
from concourse import mybir
import numpy as np

F32 = mybir.dt.float32
BF16 = mybir.dt.bfloat16
I32 = mybir.dt.int32
U8 = mybir.dt.uint8
ALU = mybir.AluOpType
ACT = mybir.ActivationFunctionType
AX = mybir.AxisListType

B, T, H, C = 8, 128, 256, 128
P = 128
PAIRS = B // 2
NH = 16
DS, DC, DM = 16, 8, 64
FF = 688
FFC = -(-FF // P)
FFP = FFC * P
FFL = FF - (FFC - 1) * P
INNER = NH * DM
MC = INNER // P
GROUPS = 4
UNITS = [(g, j) for g in range(GROUPS) for j in range(2)]
ATT = {"self": 0, "cross": 1, "media": 2}
POOL_SETUP, SMALL, DVE_LINKS = 7, 10, 75
LAG_T, LAG_V, LAG_N = 2, 3, 4
NEG = -1e30

C_ID, C_CAUSAL, C_EO, C_M4, C_COS, C_SIN, C_IOTA, C_END = np.cumsum([0, P, P, 2, 4, DS, DS, 1]).tolist()


def constants():
    c = np.zeros((P, C_END), np.float32)
    p = np.arange(P)
    c[:, C_ID:C_ID + P] = np.eye(P)
    c[:, C_CAUSAL:C_CAUSAL + P] = np.where(p[None, :] > p[:, None], NEG, 0)
    c[:, C_EO:C_EO + 2] = (p[:, None] % 32) // DS == np.arange(2)
    c[:, C_M4:C_M4 + 4] = (p[:, None] % 32) // DC == np.arange(4)
    inv = np.float32(1.0) / np.float32(10000.0) ** (np.arange(0, DS, 2, dtype=np.float32) / np.float32(DS))
    f = np.outer(np.arange(T, dtype=np.float32), inv).astype(np.float32)
    c[:, C_COS:C_COS + DS] = np.cos(np.concatenate([f, f], 1))
    c[:, C_SIN:C_SIN + DS] = np.sin(np.concatenate([-f, f], 1))
    c[:, C_IOTA] = p
    return c


def psum_plan():
    rings = {"T": [0, 1], "S": [2, 3, 4], "M": [5, 6, 7]}
    order = []

    def attention(a):
        for n in range(len(UNITS) + LAG_N):
            if n < len(UNITS):
                order.append(("S", (a, "score", n)))
            if 0 <= n - LAG_T < len(UNITS):
                order.append(("T", (a, "pT", n - LAG_T)))
            if 0 <= n - LAG_V < len(UNITS):
                order.append(("M", (a, "pv", n - LAG_V)))

    def both(ring, *names):
        for j in range(2):
            for n in names:
                order.append((ring, (n, j)))

    def memory(k):
        both("T", f"m{k}.xT")
        both("S", f"m{k}.score")
        both("T", f"m{k}.pT")
        both("M", f"m{k}.mc")
        both("T", f"m{k}.mcT")
        both("M", f"m{k}.gate")

    order += [("T", ("encT",))]
    order += [("M", ("ck",)), ("M", ("cv",)), ("M", ("m0.mpT",)), ("M", ("m0.mp",))]
    both("T", "xT")
    both("M", "qk", "v")
    both("T", "qkT")
    attention("self")
    both("T", "oT")
    both("M", "dense")
    both("T", "ciT")
    order.append(("M", ("cq",)))
    attention("cross")
    both("T", "coT")
    both("M", "cdense")
    order += [("M", ("k2", c)) for c in range(4)]
    both("T", "miT")
    order += [("M", ("ffn", i)) for i in range(FFC)]
    both("M", "down")
    memory(0)
    for j in range(2):
        order += [("M", ("v2", j, h)) for h in range(2)]
    both("T", "qnT")
    order += [("M", ("q2", c)) for c in range(4)]
    attention("media")
    for h in range(2):
        for j in range(2):
            order.append(("T", ("o2T", j, h)))
    both("M", "wo")
    order += [("M", ("m1.mpT",)), ("M", ("m1.mp",))]
    both("T", "hnT")
    order += [("M", ("ff2", c)) for c in range(4)]
    both("M", "w2")
    memory(1)

    used = {k: 0 for k in rings}
    per_bank = {b: 0 for r in rings.values() for b in r}
    plan = {}
    for ring, name in order:
        bank = rings[ring][used[ring] % len(rings[ring])]
        used[ring] += 1
        assert name not in plan
        plan[name] = (bank, per_bank[bank])
        per_bank[bank] += 1
    return order, plan, per_bank


def build(nc, t, out):
    order, plan, per_bank = psum_plan()
    with ExitStack() as ctx:
        def sb(name, shape, dt=F32):
            return ctx.enter_context(nc.sbuf_tensor(name, shape, dt))

        def sem(name):
            return ctx.enter_context(nc.semaphore(name))

        cst = sb("cst", [P, C_END])
        ident = cst[:, C_ID:C_ID + P]
        identb = sb("identb", [P, P], BF16)
        causal = sb("causal", [P, 4, P], BF16)
        onesb = sb("onesb", [1, P], BF16)
        onesf = sb("onesf", [1, P])
        minus_half = sb("minus_half", [P, 1])
        w_qkv = sb("w_qkv", [P, 2, 2, 3 * H])
        w_dense = sb("w_dense", [P, 2, 2 * H])
        w_cq = sb("w_cq", [P, 2, C])
        w_ckv = sb("w_ckv", [P, 2 * C])
        w_cdense = sb("w_cdense", [P, H])
        w_gu = sb("w_gu", [P, 2, 2, 2, FFP])
        w_down = sb("w_down", [P, FFC, 2 * H])
        w_memT = sb("w_memT", [P, 2, H])
        w_gateT = sb("w_gateT", [P, 2, 4, H])
        b_gate = sb("b_gate", [1, 2, H])
        norm_w = sb("norm_w", [P, 2, H])
        w_q2 = sb("w_q2", [P, 2, INNER])
        w_kv2 = sb("w_kv2", [P, 2 * INNER])
        w_o2 = sb("w_o2", [P, MC, H])
        w_1 = sb("w_1", [P, 2, INNER])
        w_2 = sb("w_2", [P, MC, H])
        cols = sb("cols", [P, 7, 2])
        LN_IN, LN_CROSS, LN_ATTN, Q_G, Q_B, FF_G, FF_B = range(7)
        gates = sb("gates", [P, 2])
        tgates = sb("tgates", [P, 2])
        pos_i = sb("pos_i", [P, T], I32)
        pos_f = sb("pos_f", [P, 2, T])
        rope = sb("rope", [P, 2 * DS])
        tt_i = sb("tt_i", [P, 2, B], I32)
        tt_f = sb("tt_f", [P, 2, B])
        vm_all = sb("vm_all", [P, 2, B])

        x_in = sb("x_in", [P, 2, H])
        enc = sb("enc", [P, 2, C])
        mm_u8 = sb("mm_u8", [1, 2, T], U8)
        vm = sb("vm", [P, 2, 2])
        mrow = sb("mrow", [1, 2, 4, T], BF16)
        encT = sb("encT", [P, 2, T])
        var = sb("var", [P, 7, 2, 2])
        vare = sb("vare", [P, 7, 2])
        rstd = sb("rstd", [P, 7, 2])
        bns = sb("bns", [P, 2, 6])
        xs = sb("xs", [P, 2, 2, H])
        xT = sb("xT", [P, 2, 2, 2, T])
        v_self = sb("v_self", [P, 2, NH, DS + 1])
        v_cross = sb("v_cross", [P, 2, NH, DC + 1])
        v_media = sb("v_media", [P, 2, NH, DM + 1])
        mx = sb("mx", [P, 3, 4])
        pr = sb("pr", [P, 3, 4 * P])
        pT = sb("pT", [P, 2, 4 * P])
        rec = sb("rec", [P, 2, 4])
        on = sb("on", [P, 2, INNER])
        oT = sb("oT", [P, 2, 2, T])
        x1 = x3 = x5 = sb("x135", [P, 2, H])
        x2 = x4 = x6 = sb("x246", [P, 2, H])
        y = sb("y", [P, 2, H])
        xn = sb("xn", [P, 2, H])
        nT = sb("nT", [P, 2, 2, T])
        th = sb("th", [P, 2, 2 * T])
        tg = sb("tg", [P, 2, 2 * T])
        mpT = sb("mpT", [P, 2, 2, T])
        mp = sb("mp", [P, 2, H])
        mmx = sb("mmx", [P, 2, 4])
        mpr = sb("mpr", [P, 2, T])
        mpr_T = sb("mpr_T", [P, 2, T])
        mc = sb("mc", [P, 2, H])
        gth = sb("gth", [P, 2, H])
        fus = sb("fus", [P, 2, H])
        big_q = sb("big_q", [P, MC * 2 * T])
        big_k = sb("big_k", [P, MC * 2 * T])
        qT2 = big_q[:, :].rearrange("p (c j t) -> p c j t", j=2, t=T)
        h2T = qT2
        ckm = big_q[:, 0:8 * T].rearrange("p (j h t) -> p j h t", j=2, h=4)
        cqT = big_q[:, 8 * T:10 * T].rearrange("p (j t) -> p j t", j=2)
        kT2 = big_k[:, :].rearrange("p (c j t) -> p c j t", j=2, t=T)
        o2T = big_k[:, :].rearrange("p (j c t) -> p j c t", j=2, c=MC)
        keo = big_k[:, 0:8 * T].rearrange("p (j a e t) -> p j a e t", j=2, a=2, e=2)
        qT = big_k[:, 8 * T:12 * T].rearrange("p (j a t) -> p j a t", j=2, a=2)
        rot = on[:, :, 0:2 * H]
        rot2 = on[:, :, 2 * H:4 * H]
        hT = pr[:, :, :].rearrange("p a n -> p (a n)").rearrange("p (i j t) -> p i j t", j=2, t=T)
        lT = xT[:, :, :, :, :].rearrange("p c e j t -> p (c e j t)").rearrange("p (j c t) -> p j c t", j=2, c=4)
        bank = [ctx.enter_context(nc.psum_tensor(f"bank{k}", [P, 512], F32)) for k in range(8)]

        filled = [sem(f"filled{k}") for k in range(8)]
        drained = [sem(f"drained{k}") for k in range(8)]
        loaded = {n: sem(f"loaded_{n}") for n in ("const", "small", "m", "self", "cross", "kv2", "ffn", "down", "q2",
                                                  "o2", "ff2")}
        x_loaded, enc_loaded, mask_loaded, y_stored = (sem(n) for n in ("x_loaded", "enc_loaded", "mask_loaded", "y_stored"))
        pads_zero = sem("pads_zero")
        pool_setup, dve_setup, pe_setup, act_setup = (sem(f"{n}_setup") for n in ("pool", "dve", "pe", "act"))
        dve_chain = sem("dve_chain")
        pool_chain = sem("pool_chain")
        passed_pool, passed_dve = sem("passed_pool"), sem("passed_dve")
        var_ready = [sem(f"var_ready{n}") for n in range(7)]
        rstd_ready = [sem(f"rstd_ready{n}") for n in range(7)]
        ready = {n: sem(f"{n}_ready") for n in ("masks", "onehot", "mrow", "xs", "rot", "probs", "xn", "tanh", "mneg",
                                                "fused", "x4", "y")}
        block = ctx.enter_context(nc.Block())

        def at(it, per, k):
            return it * per + k

        def wait_filled(eng, it, name):
            b, k = plan[name]
            eng.wait_ge(filled[b], at(it, per_bank[b], k + 1))
            return bank[b]

        def wait_evacuated(eng, it, name):
            b, k = plan[name]
            eng.wait_ge(drained[b], at(it, per_bank[b], k + 2))

        def gone(name):
            return drained[plan[name][0]]

        xd = t["x"].rearrange("b t h -> t b h")
        cd = t["ctx_1024"].rearrange("b t h -> t b h")
        od = out.rearrange("b t h -> t b h")

        def chunks(a):
            return a.rearrange("(c p) n -> p c n", p=P)

        def column(a):
            return a.rearrange("(c p) -> p c", p=P)

        NORMS = [(1 / H, 1e-6)] * 4 + [(1.0, 1e-5)] * 2 + [(1 / H, 1e-6)]
        N_IN, N_CROSS, N_ATTN, N_M0, N_Q, N_FF, N_M1 = range(7)
        XN = {"ci": 0, "qn": 1, "hn": 2}
        BLOCKS = {0: (x3, x4, N_M0), 1: (x6, y, N_M1)}

        @block.sync
        def _(sp):
            def get(group, to, source):
                sp.dma_start(to, source).then_inc(loaded[group], 16)

            def load_pair(i):
                sp.dma_start(enc[:], cd[:, bass.ds(i * 2, 2), :]).then_inc(enc_loaded, 16)
                sp.dma_start(x_in[:], xd[:, bass.ds(i * 2, 2), :]).then_inc(x_loaded, 16)
                sp.dma_start(mm_u8[:], t["mask_BxS2_bk0"][bass.ds(i * 2, 2), :].rearrange("(o b) t -> o b t", o=1))\
                    .then_inc(mask_loaded, 16)

            get("const", cst[:], t["constants"])
            load_pair(0)
            for k, b in enumerate((1, 3)):
                get("m", w_memT[:, k, :], t[f"L{b}_xattn_W_mem"])
                get("m", w_gateT[:, k], chunks(t[f"L{b}_xattn_W_gate"]))
            get("cross", w_ckv[:], t["L0_xattn_ckv_w"])
            get("self", w_qkv[:, 0], chunks(t["L0_xattn_v_qkv"]))
            get("self", w_qkv[:, 1], chunks(t["L0_xattn_l_qkv"]))
            get("self", w_dense[:, :, 0:H], chunks(t["L0_xattn_v_dense"]))
            get("self", w_dense[:, :, H:2 * H], chunks(t["L0_xattn_l_dense"]))
            get("cross", w_cq[:], chunks(t["L0_xattn_cq_w"]))
            get("cross", w_cdense[:], t["L0_xattn_cdense_w"])
            get("kv2", w_kv2[:], t["L2_xattn_Wkv"])
            sp.wait_ge(pads_zero, 2)
            for e, n in enumerate("vl"):
                for k, g in enumerate(("gate", "up")):
                    get("ffn", w_gu[:, e, :, k, 0:FF], chunks(t[f"L0_xattn_{n}_{g}"]))
            for e, n in enumerate("vl"):
                w = t[f"L0_xattn_{n}_down"]
                get("down", w_down[:, 0:FFC - 1, e * H:(e + 1) * H], chunks(w[0:(FFC - 1) * P, :]))
                get("down", w_down[0:FFL, FFC - 1, e * H:(e + 1) * H], w[(FFC - 1) * P:FF, :])
            get("q2", w_q2[:], chunks(t["L2_xattn_Wq"]))
            get("o2", w_o2[:], chunks(t["L2_xattn_Wo"]))
            get("ff2", w_1[:], chunks(t["L2_xattn_W1"]))
            get("ff2", w_2[:], chunks(t["L2_xattn_W2"]))

            def store_pair(i):
                sp.wait_ge(ready["y"], at(i, 2, 2))
                sp.dma_start(od[:, bass.ds(i * 2, 2), :], y[:]).then_inc(y_stored, 16)

            with sp.Fori(0, PAIRS - 1) as it:
                wait_filled(sp, it, ("encT",))
                wait_evacuated(sp, it, ("dense", 1))
                load_pair(it + 1)
                store_pair(it)
            store_pair(PAIRS - 1)
            sp.wait_ge(y_stored, 16 * PAIRS + 16)

        @block.gpsimd
        def _(pool):
            nc.gpsimd.memset(w_down[:, FFC - 1, :], 0.0).then_inc(pads_zero, 1)
            nc.gpsimd.memset(w_gu[:, :, :, :, FF:FFP].rearrange("p e c k n -> p (e c k) n"), 0.0).then_inc(pads_zero, 1)
            nc.gpsimd.memset(tt_i[:, 1, :], 0).then_inc(pool_setup, 1)
            nc.gpsimd.memset(onesb[:], 1.0).then_inc(pool_setup, 1)
            nc.gpsimd.memset(onesf[:], 1.0).then_inc(pool_setup, 1)
            nc.gpsimd.memset(minus_half[:], -0.5).then_inc(pool_setup, 1)
            nc.gpsimd.memset(v_self[:], 1.0).then_inc(pool_setup, 1)
            nc.gpsimd.memset(v_cross[:], 1.0).then_inc(pool_setup, 1)
            nc.gpsimd.memset(v_media[:], 1.0).then_inc(pool_setup, 1)

            def get(to, source):
                pool.dma_start(to, source).then_inc(loaded["small"], 16)

            get(pos_i[:], t["pos_1xS"][0].partition_broadcast(P))
            get(tt_i[:, 0, :], t["types_T"])
            pool.wait_ge(pool_setup, POOL_SETUP)
            get(tt_i[0:T - 1, 1, :], t["types_T"][1:T, :])
            get(cols[:].rearrange("p k c -> p (k c)"), t["columns"])
            get(gates[:, 0:1], t["L2_xattn_attn_gate"].partition_broadcast(P))
            get(gates[:, 1:2], t["L2_xattn_ff_gate"].partition_broadcast(P))
            for k, b in enumerate((1, 3)):
                get(b_gate[:, k, :], t[f"L{b}_xattn_b_gate"].rearrange("(o n) -> o n", o=1))
                get(norm_w[:, k, :], t[f"L{b}_xattn_norm_w"].partition_broadcast(P))

            def inverse_root(it, n, j):
                scale, eps = NORMS[n]
                pool.wait_ge(var_ready[n], at(it, 2, j + 1))
                pool.sem_inc(passed_pool, 1)
                nc.gpsimd.tensor_scalar(vare[:, n, j:j + 1], var[:, n, j, 1:2], scale, eps, ALU.mult,
                                        ALU.add).then_inc(pool_chain, 1)
                pool.wait_ge(pool_chain, at(it, 14, n * 2 + j + 1))
                nc.gpsimd.tensor_tensor(rstd[:, n, j:j + 1], vare[:, n, j:j + 1], minus_half[:],
                                        ALU.pow).then_inc(rstd_ready[n], 1)

            with pool.Fori(0, PAIRS) as it:
                for n in range(len(NORMS)):
                    for j in range(2):
                        inverse_root(it, n, j)

        @block.scalar
        def _(act):
            copy, exp, tanh = ACT.Copy, ACT.Exp, ACT.Tanh
            act.wait_ge(loaded["small"], 16 * SMALL)
            nc.scalar.activation(tgates[:], gates[:], tanh).then_inc(act_setup, 1)

            def evacuate(it, name, out, of=lambda b: b[:, :], func=copy, **kw):
                b = wait_filled(act, it, name)
                nc.scalar.activation(out, of(b), func, **kw).then_inc(gone(name), 1)

            def squares(it, n, j, x):
                nc.scalar.activation((mc if n == N_IN else gth)[:, j, :], x[:, j, :], ACT.Square,
                                     accum_out=var[:, n, j, 1:2]).then_inc(var_ready[n], 1)

            def attention(it, a):
                for n in range(len(UNITS) + LAG_T):
                    if n >= LAG_T:
                        m = n - LAG_T
                        evacuate(it, (a, "pT", m), pT[:, m % 2, :])
                    if n < len(UNITS):
                        wait_evacuated(act, it, (a, "score", n))
                        nc.scalar.activation(pr[:, n % 3, :], pr[:, n % 3, :], exp).then_inc(ready["probs"], 1)

            def memory(it, k):
                src, dst, norm = BLOCKS[k]
                for j in range(2):
                    evacuate(it, (f"m{k}.xT", j), lT[:, j, 0:2, :].rearrange("p c t -> p (c t)"), lambda b: b[:, 0:2 * T])
                for j in range(2):
                    b = wait_filled(act, it, (f"m{k}.score", j))
                    act.wait_ge(ready["mneg"], at(it, 4, 2 * k + j + 1))
                    nc.scalar.activation(mpr[:, j, :], b[:, 0:T], exp, bias=mmx[:, j, 1:2], scale=H ** -0.5,
                                         accum_out=mmx[:, j, 2:3]).then_inc(gone((f"m{k}.score", j)), 1)
                for j in range(2):
                    evacuate(it, (f"m{k}.pT", j), mpr_T[:, j, :], lambda b: b[:, 0:T])
                for j in range(2):
                    evacuate(it, (f"m{k}.mcT", j), lT[:, j, 2:4, :].rearrange("p c t -> p (c t)"), lambda b: b[:, 0:2 * T])
                for j in range(2):
                    evacuate(it, (f"m{k}.gate", j), gth[:, j, :], lambda b: b[:, 0:H], tanh, scale=0.5)
                for j in range(2):
                    act.wait_ge(ready["fused"], at(it, 4, 2 * k + j + 1))
                    squares(it, norm, j, fus)

            def scaled_T(it, name, j, k, out, shift=None):
                b = wait_filled(act, it, (name, j))
                for c in range(2):
                    kw = {"bias": cols[:, shift, c:c + 1]} if shift is not None else {}
                    w = b.shape[1] // 2 if name in ("xT", "miT") else T
                    i = nc.scalar.activation(out(c), b[:, c * w:(c + 1) * w], ACT.Identity if kw else copy,
                                             scale=cols[:, k, c:c + 1], **kw)
                i.then_inc(gone((name, j)), 1)

            with act.Fori(0, PAIRS) as it:
                act.wait_ge(x_loaded, at(it, 16, 16))
                for j in range(2):
                    squares(it, N_IN, j, x_in)
                evacuate(it, ("encT",), encT[:].rearrange("p j t -> p (j t)"), lambda b: b[:, 0:2 * T])
                evacuate(it, ("cv",), v_cross[:, :, :, 0:DC],
                         lambda b: b[:, 0:2 * C].rearrange("p (j h d) -> p j h d", j=2, h=NH))
                evacuate(it, ("m0.mpT",), mpT[:].rearrange("p c j t -> p (c j t)"))
                for j in range(2):
                    scaled_T(it, "xT", j, LN_IN, lambda c: xT[:, c, :, j, :])
                for j in range(2):
                    evacuate(it, ("v", j), v_self[:, j, :, 0:DS],
                             lambda b: b[:, 0:H].rearrange("p (h d) -> p h d", h=NH))
                for j in range(2):
                    b = wait_filled(act, it, ("qkT", j))
                    nc.scalar.activation(qT[:, j].rearrange("p g t -> p (g t)"), b[:, 0:2 * T], copy, scale=DS ** -0.5)
                    for e in range(2):
                        i = nc.scalar.activation(keo[:, j, :, e, :], b[:, 2 * T:].rearrange("p (g t) -> p g t", g=2), copy,
                                                 scale=cst[:, C_EO + e:C_EO + e + 1])
                    i.then_inc(gone(("qkT", j)), 1)
                attention(it, "self")
                for j in range(2):
                    evacuate(it, ("oT", j), oT[:, j].rearrange("p c t -> p (c t)"), lambda b: b[:, 0:2 * T])
                for j in range(2):
                    wait_evacuated(act, it, ("dense", j))
                    squares(it, N_CROSS, j, x1)
                for j in range(2):
                    scaled_T(it, "ciT", j, LN_CROSS, lambda c: nT[:, c, j, :])
                evacuate(it, ("cq",), cqT[:].rearrange("p j t -> p (j t)"), lambda b: b[:, 0:2 * T], scale=DC ** -0.5)
                attention(it, "cross")
                for j in range(2):
                    evacuate(it, ("coT", j), oT[:, j, 0, :], lambda b: b[:, 0:T])
                for j in range(2):
                    wait_evacuated(act, it, ("cdense", j))
                    squares(it, N_ATTN, j, x2)
                for j in range(2):
                    scaled_T(it, "miT", j, LN_ATTN, lambda c: xT[:, c, :, j, :])
                for i in range(FFC):
                    b = wait_filled(act, it, ("ffn", i))
                    if i >= 2:
                        wait_evacuated(act, it, ("ffn", i - 2))
                    nc.scalar.activation(th[:, i % 2, :], b[:, 0:2 * T], tanh, scale=0.5).then_inc(ready["tanh"], 1)
                memory(it, 0)
                for j in range(2):
                    for h in range(2):
                        evacuate(it, ("v2", j, h), v_media[:, j, h * 8:h * 8 + 8, 0:DM],
                                 lambda b: b[:, :].rearrange("p (h d) -> p h d", h=8))
                for j in range(2):
                    scaled_T(it, "qnT", j, Q_G, lambda c: nT[:, c, j, :], Q_B)
                for c in range(4):
                    evacuate(it, ("q2", c), qT2[:, 2 * c:2 * c + 2].rearrange("p c j t -> p (c j t)"), scale=DM ** -0.5)
                attention(it, "media")
                for j in range(2):
                    evacuate(it, ("o2T", j, 0), o2T[:, j, 0:4, :].rearrange("p c t -> p (c t)"))
                evacuate(it, ("m1.mpT",), mpT[:].rearrange("p c j t -> p (c j t)"))
                for j in range(2):
                    scaled_T(it, "hnT", j, FF_G, lambda c: nT[:, c, j, :], FF_B)
                for c in range(4):
                    evacuate(it, ("ff2", c), h2T[:, 2 * c:2 * c + 2].rearrange("p c j t -> p (c j t)"), func=ACT.Gelu)
                memory(it, 1)

        @block.vector
        def _(dve):
            chained = [0]

            def link(it, ins):
                chained[0] += 1
                ins.then_inc(dve_chain, 1)
                dve.wait_ge(dve_chain, at(it, DVE_LINKS, chained[0]))

            steps = [0]

            def step(ins):
                steps[0] += 1
                ins.then_inc(dve_setup, 1)
                dve.wait_ge(dve_setup, steps[0])

            dve.wait_ge(loaded["const"], 16)
            nc.vector.tensor_copy(identb[:], ident).then_inc(ready["masks"], 1)
            nc.vector.tensor_copy(causal[:], cst[:, C_CAUSAL:C_CAUSAL + P].unsqueeze(1).broadcast_to([P, 4, P]))\
                .then_inc(ready["masks"], 1)
            dve.wait_ge(loaded["small"], 16 * SMALL)
            pf, pg = pos_f[:, 0, :], pos_f[:, 1, :]
            step(nc.vector.tensor_copy(pf, pos_i[:]))
            step(nc.vector.tensor_scalar(pg, pf, 0.0, float(T), ALU.is_lt, ALU.mult))
            step(nc.vector.tensor_tensor(pf, pf, pg, ALU.add))
            step(nc.vector.tensor_scalar(pf, pf, 0.0, float(T - 1), ALU.max, ALU.min))
            nc.vector.tensor_scalar(pg, pf, cst[:, C_IOTA:C_IOTA + 1], None, ALU.is_equal).then_inc(ready["onehot"], 1)
            step(nc.vector.tensor_scalar(tt_f[:], tt_i[:], 1.0, None, ALU.is_equal))
            step(nc.vector.tensor_tensor(vm_all[:, 0, :], tt_f[:, 0, :], tt_f[:, 1, :], ALU.mult))
            step(nc.vector.tensor_scalar(vm_all[:, 1, :], vm_all[:, 0, :], -1.0, 1.0, ALU.mult, ALU.add))
            dve.wait_ge(pe_setup, 1)
            nc.vector.tensor_copy(rope[:], bank[5][:, 0:2 * DS]).then_inc(drained[5], 1)
            for k, a in zip((0, 1, 2, 3, 4, 6, 7), (mx[:, 0], mx[:, 1], mx[:, 2], rec[:, 0], rec[:, 1], bns[:, 0], bns[:, 1])):
                nc.vector.memset(a, 0.0).then_inc(drained[k], 1)
            nc.vector.memset(y[:], 0.0).then_inc(y_stored, 16)
            dve.wait_ge(drained[5], 1)
            dve.wait_ge(drained[6], 1)
            dve.wait_ge(drained[7], 1)
            dve.wait_ge(act_setup, 1)

            def attention(it, a, width, out):
                for n in range(len(UNITS) + LAG_N):
                    if n < len(UNITS):
                        s = wait_filled(dve, it, (a, "score", n))[:, :].rearrange("p (h k) -> p h k", h=4)
                        m = mx[:, n % 3, :]
                        link(it, nc.vector.tensor_reduce(m, s, AX.X, ALU.max))
                        nc.vector.tensor_tensor(pr[:, n % 3, :].rearrange("p (h k) -> p h k", h=4), s,
                                                m.unsqueeze(2).broadcast_to([P, 4, P]),
                                                ALU.subtract).then_inc(gone((a, "score", n)), 1)
                    if n >= LAG_N:
                        u = n - LAG_N
                        g, j = UNITS[u]
                        o = wait_filled(dve, it, (a, "pv", u))[:, 0:4 * (width + 1)].rearrange("p (h d) -> p h d", h=4)
                        r = rec[:, u % 2, :]
                        link(it, nc.vector.reciprocal(r, o[:, :, width]))
                        to = out(g, j)
                        num, den = o[:, :, 0:width], r.unsqueeze(2).broadcast_to([P, 4, width])
                        if len(to.shape) == 4:
                            num = num.rearrange("p (a b) d -> p a b d", a=2)
                            den = den.rearrange("p (a b) d -> p a b d", a=2)
                        nc.vector.tensor_tensor(to, num, den, ALU.mult).then_inc(gone((a, "pv", u)), 1)

            def by_expert(it, name, j, x, out):
                b = wait_filled(dve, it, (name, j))
                link(it, nc.vector.scalar_tensor_tensor(out[:, j, :], b[:, 0:H], vm[:, 0, j:j + 1], x[:, j, :],
                                                        ALU.mult, ALU.add))
                nc.vector.scalar_tensor_tensor(out[:, j, :], b[:, H:2 * H], vm[:, 1, j:j + 1], out[:, j, :],
                                               ALU.mult, ALU.add).then_inc(gone((name, j)), 1)

            def masked_norm(it, n, x, k):
                for j in range(2):
                    dve.wait_ge(rstd_ready[n], at(it, 2, j + 1))
                    for e in range(2):
                        i = nc.vector.tensor_scalar(xs[:, j, e, :], x[:, j, :], rstd[:, n, j:j + 1], vm[:, e, j:j + 1],
                                                    ALU.mult, ALU.mult)
                    i.then_inc(ready["xs"], 1)

            def layer_norm(it, n, x):
                for j in range(2):
                    link(it, nc.vector.bn_stats(bns[:, j, :], x[:, j, :]))
                    dve.sem_inc(passed_dve, 1)
                    nc.vector.bn_aggr(var[:, n, j, :], bns[:, j, :]).then_inc(var_ready[n], 1)
                for j in range(2):
                    dve.wait_ge(rstd_ready[n], at(it, 2, j + 1))
                    nc.vector.tensor_scalar(xn[:, j, :], x[:, j, :], var[:, n, j, 0:1], rstd[:, n, j:j + 1],
                                            ALU.subtract, ALU.mult).then_inc(ready["xn"], 1)

            def memory(it, k):
                src, dst, norm = BLOCKS[k]
                for j in range(2):
                    b = wait_filled(dve, it, (f"m{k}.score", j))
                    link(it, nc.vector.tensor_reduce(mmx[:, j, 0:1], b[:, 0:T], AX.X, ALU.max))
                    nc.vector.tensor_scalar(mmx[:, j, 1:2], mmx[:, j, 0:1], -H ** -0.5, None,
                                            ALU.mult).then_inc(ready["mneg"], 1)
                for j in range(2):
                    b = wait_filled(dve, it, (f"m{k}.mc", j))
                    link(it, nc.vector.reciprocal(mmx[:, j, 3:4], mmx[:, j, 2:3]))
                    nc.vector.tensor_scalar(mc[:, j, :], b[:, 0:H], mmx[:, j, 3:4], None,
                                            ALU.mult).then_inc(gone((f"m{k}.mc", j)), 1)
                for j in range(2):
                    wait_evacuated(dve, it, (f"m{k}.gate", j))
                    link(it, nc.vector.scalar_tensor_tensor(gth[:, j, :], gth[:, j, :], 1.0, mc[:, j, :], ALU.add,
                                                            ALU.mult))
                    nc.vector.scalar_tensor_tensor(fus[:, j, :], gth[:, j, :], 0.5, src[:, j, :], ALU.mult,
                                                   ALU.add).then_inc(ready["fused"], 1)
                if k == 1:
                    with_store(it)
                for j in range(2):
                    dve.wait_ge(rstd_ready[norm], at(it, 2, j + 1))
                    nc.vector.scalar_tensor_tensor(dst[:, j, :], fus[:, j, :], rstd[:, norm, j:j + 1], norm_w[:, k, :],
                                                   ALU.mult, ALU.mult).then_inc(ready["y" if k else "x4"], 1)

            def with_store(it):
                dve.wait_ge(y_stored, at(it, 16, 16))

            with dve.Fori(0, PAIRS) as it:
                link(it, nc.vector.tensor_copy(vm[:], vm_all[:, :, bass.ds(it * 2, 2)]))
                dve.wait_ge(mask_loaded, at(it, 16, 16))
                nc.vector.tensor_scalar(mrow[:], mm_u8[:].unsqueeze(2).broadcast_to([1, 2, 4, T]), -NEG, NEG, ALU.mult,
                                        ALU.add).then_inc(ready["mrow"], 1)
                b = wait_filled(dve, it, ("ck",))
                nc.vector.tensor_tensor(
                    ckm[:], b[:, 0:2 * T].rearrange("p (j t) -> p j t", j=2).unsqueeze(2).broadcast_to([P, 2, 4, T]),
                    cst[:, C_M4:C_M4 + 4].unsqueeze(1).unsqueeze(3).broadcast_to([P, 2, 4, T]),
                    ALU.mult).then_inc(gone(("ck",)), 1)
                b = wait_filled(dve, it, ("m0.mp",))
                nc.vector.tensor_copy(mp[:].rearrange("p j n -> p (j n)"), b[:, :]).then_inc(gone(("m0.mp",)), 1)
                masked_norm(it, N_IN, x_in, 0)
                for j in range(2):
                    b = wait_filled(dve, it, ("qk", j))[:, :].rearrange("p (h s d) -> p h s d", h=2 * NH, s=2)
                    r1 = rot[:, j, :].rearrange("p (h d) -> p h d", d=DS)
                    r2 = rot2[:, j, :].rearrange("p (h s d) -> p h s d", h=2 * NH, s=2)
                    nc.vector.tensor_tensor(r1, b.rearrange("p h s d -> p h (s d)"),
                                            rope[:, 0:DS].unsqueeze(1).broadcast_to([P, 2 * NH, DS]), ALU.mult)
                    for s in range(2):
                        i = nc.vector.tensor_tensor(
                            r2[:, :, s, :], b[:, :, 1 - s, :],
                            rope[:, DS + 8 * s:DS + 8 * s + 8].unsqueeze(1).broadcast_to([P, 2 * NH, DS // 2]), ALU.mult)
                    i.then_inc(gone(("qk", j)), 1)
                    wait_evacuated(dve, it, ("qk", j))
                    nc.vector.tensor_tensor(rot[:, j, :], rot[:, j, :], rot2[:, j, :], ALU.add).then_inc(ready["rot"], 1)
                attention(it, "self", DS, lambda g, j: on[:, j, 0:H].rearrange("p (a g e d) -> p a g e d", a=2, g=4, e=2)[:, :, g])
                for j in range(2):
                    by_expert(it, "dense", j, x_in, x1)
                for j in range(2):
                    dve.wait_ge(rstd_ready[N_CROSS], at(it, 2, j + 1))
                    nc.vector.tensor_scalar(xn[:, j, :], x1[:, j, :], rstd[:, N_CROSS, j:j + 1], None,
                                            ALU.mult).then_inc(ready["xn"], 1)
                attention(it, "cross", DC, lambda g, j: on[:, j, g * 4 * DC:(g + 1) * 4 * DC].rearrange("p (h d) -> p h d", h=4))
                for j in range(2):
                    b = wait_filled(dve, it, ("cdense", j))
                    nc.vector.tensor_tensor(x2[:, j, :], b[:, 0:H], x1[:, j, :], ALU.add).then_inc(gone(("cdense", j)), 1)
                for c in range(4):
                    b = wait_filled(dve, it, ("k2", c))
                    nc.vector.tensor_copy(kT2[:, 2 * c:2 * c + 2].rearrange("p c j t -> p (c j t)"), b[:, :])\
                        .then_inc(gone(("k2", c)), 1)
                masked_norm(it, N_ATTN, x2, 1)
                for i in range(FFC):
                    b = wait_filled(dve, it, ("ffn", i))
                    dve.wait_ge(ready["tanh"], at(it, FFC, i + 1))
                    link(it, nc.vector.scalar_tensor_tensor(tg[:, i % 2, :], th[:, i % 2, :], 1.0, b[:, 0:2 * T],
                                                            ALU.add, ALU.mult))
                    nc.vector.scalar_tensor_tensor(hT[:, i].rearrange("p j t -> p (j t)"), tg[:, i % 2, :], 0.5,
                                                   b[:, 2 * T:], ALU.mult, ALU.mult).then_inc(gone(("ffn", i)), 1)
                for j in range(2):
                    by_expert(it, "down", j, x2, x3)
                memory(it, 0)
                dve.wait_ge(ready["x4"], at(it, 2, 2))
                layer_norm(it, N_Q, x4)
                attention(it, "media", DM, lambda g, j: on[:, j, :].rearrange("p (a c e d) -> p a c e d", a=2, c=4, e=2)
                          [:, g // 2, :, g % 2, :])
                for j in range(2):
                    b = wait_filled(dve, it, ("o2T", j, 1))
                    nc.vector.tensor_copy(o2T[:, j, 4:8, :].rearrange("p c t -> p (c t)"), b[:, :])\
                        .then_inc(gone(("o2T", j, 1)), 1)
                for j in range(2):
                    b = wait_filled(dve, it, ("wo", j))
                    nc.vector.scalar_tensor_tensor(x5[:, j, :], b[:, 0:H], tgates[:, 0:1], x4[:, j, :], ALU.mult,
                                                   ALU.add).then_inc(gone(("wo", j)), 1)
                b = wait_filled(dve, it, ("m1.mp",))
                nc.vector.tensor_copy(mp[:].rearrange("p j n -> p (j n)"), b[:, :]).then_inc(gone(("m1.mp",)), 1)
                wait_evacuated(dve, it, ("wo", 1))
                layer_norm(it, N_FF, x5)
                for j in range(2):
                    b = wait_filled(dve, it, ("w2", j))
                    nc.vector.scalar_tensor_tensor(x6[:, j, :], b[:, 0:H], tgates[:, 1:2], x5[:, j, :], ALU.mult,
                                                   ALU.add).then_inc(gone(("w2", j)), 1)
                memory(it, 1)
            assert chained[0] == DVE_LINKS, chained

        @block.tensor
        def _(pe):
            mm = nc.tensor.matmul

            pe.wait_ge(ready["onehot"], 1)
            mm(bank[5][:, 0:2 * DS], pos_f[:, 1, :], cst[:, C_COS:C_COS + 2 * DS], start=True, stop=True)\
                .then_inc(pe_setup, 1)
            pe.wait_ge(ready["masks"], 2)
            pe.wait_ge(pool_setup, POOL_SETUP)

            def fill(it, name):
                b, k = plan[name]
                pe.wait_ge(drained[b], at(it, per_bank[b], k + 1))
                return bank[b]

            def done(ins, name):
                ins.then_inc(filled[plan[name][0]], 1)

            def turn(it, name, sources):
                b = fill(it, name)
                for k, s in enumerate(sources):
                    i = nc.tensor.transpose(b[:, k * P:(k + 1) * P], s, ident)
                done(i, name)

            def attention(it, a, scores, values, width):
                for n in range(len(UNITS) + LAG_V):
                    if n < len(UNITS):
                        g, j = UNITS[n]
                        b = fill(it, (a, "score", n))
                        done(scores(b, g, j), (a, "score", n))
                    m = n - LAG_T
                    if 0 <= m < len(UNITS):
                        pe.wait_ge(ready["probs"], at(it, 3 * len(UNITS), ATT[a] * len(UNITS) + m + 1))
                        turn(it, (a, "pT", m), [pr[:, m % 3, h * P:(h + 1) * P] for h in range(4)])
                    m = n - LAG_V
                    if 0 <= m < len(UNITS):
                        g, j = UNITS[m]
                        wait_evacuated(pe, it, (a, "pT", m))
                        b = fill(it, (a, "pv", m))
                        for h in range(4):
                            i = mm(b[:, h * (width + 1):(h + 1) * (width + 1)], pT[:, m % 2, h * P:(h + 1) * P],
                                   values(g, j, h), start=True, stop=True)
                        done(i, (a, "pv", m))

            def memory(it, k):
                src, dst, norm = BLOCKS[k]
                for j in range(2):
                    wait_evacuated(pe, it, (("down", "w2")[k], j))
                    turn(it, (f"m{k}.xT", j), [src[:, j, c * P:(c + 1) * P] for c in range(2)])
                for j in range(2):
                    wait_evacuated(pe, it, (f"m{k}.xT", j))
                    b = fill(it, (f"m{k}.score", j))
                    for c in range(2):
                        i = mm(b[:, 0:T], lT[:, j, c, :], mpT[:, c, j, :], start=c == 0, stop=c == 1)
                    done(i, (f"m{k}.score", j))
                for j in range(2):
                    wait_evacuated(pe, it, (f"m{k}.score", j))
                    turn(it, (f"m{k}.pT", j), [mpr[:, j, :]])
                for j in range(2):
                    wait_evacuated(pe, it, (f"m{k}.pT", j))
                    b = fill(it, (f"m{k}.mc", j))
                    done(mm(b[:, 0:H], mpr_T[:, j, :], mp[:, j, :], start=True, stop=True), (f"m{k}.mc", j))
                for j in range(2):
                    wait_evacuated(pe, it, (f"m{k}.mc", j))
                    turn(it, (f"m{k}.mcT", j), [mc[:, j, c * P:(c + 1) * P] for c in range(2)])
                for j in range(2):
                    wait_evacuated(pe, it, (f"m{k}.mcT", j))
                    b = fill(it, (f"m{k}.gate", j))
                    for c in range(4):
                        mm(b[:, 0:H], lT[:, j, c, :], w_gateT[:, k, c, :], start=c == 0, stop=False)
                    done(mm(b[:, 0:H], onesf[:], b_gate[:, k, :], start=False, stop=True), (f"m{k}.gate", j))

            def memory_projections(it, k):
                name = (f"m{k}.mpT",)
                pe.wait_ge(loaded["m"], 16 * 4)
                b = fill(it, name)
                for c in range(2):
                    i = mm(b[:, c * 2 * T:(c + 1) * 2 * T], w_memT[:, k, c * P:(c + 1) * P],
                           encT[:].rearrange("p j t -> p (j t)"), start=True, stop=True)
                done(i, name)
                name = (f"m{k}.mp",)
                b = fill(it, name)
                for j in range(2):
                    i = mm(b[:, j * H:(j + 1) * H], encT[:, j, :], w_memT[:, k, :], start=True, stop=True)
                done(i, name)

            def from_both(it, name, w, x, chunks_out, n_in):
                b = fill(it, name)
                for o in chunks_out:
                    for c in range(n_in):
                        at_ = b[:, (o - chunks_out[0]) * 2 * T:(o - chunks_out[0] + 1) * 2 * T]
                        i = mm(at_, w(c, o), x(c), start=c == 0, stop=c == n_in - 1)
                done(i, name)

            def both(x):
                return x.rearrange("p j t -> p (j t)")

            def score_self(b, g, j):
                r = slice(32 * g, 32 * g + 32)
                for a in range(2):
                    mm(b[:, a * 2 * P:(a + 1) * 2 * P], qT[r, j, a, :], keo[r, j, a].rearrange("p e t -> p (e t)"),
                       start=a == 0, stop=False, skip_group_check=True)
                return mm(b[:, :], identb[:], causal[:].rearrange("p h k -> p (h k)"), start=False, stop=True,
                          skip_group_check=True)

            def score_cross(b, g, j):
                r = slice(32 * g, 32 * g + 32)
                return mm(b[:, :], cqT[r, j, :], ckm[r, j].rearrange("p h t -> p (h t)"), start=True, stop=True)

            def score_media(b, g, j):
                r = slice(64 * (g % 2), 64 * (g % 2) + 64)
                for h in range(4):
                    c = g // 2 * 4 + h
                    mm(b[:, h * P:(h + 1) * P], qT2[r, c, j, :], kT2[r, c, j, :], start=h == 0, stop=False,
                       skip_group_check=True)
                return mm(b[:, :], onesb[:], mrow[:, j].rearrange("p h t -> p (h t)"), start=False, stop=True,
                          skip_group_check=True)

            def norm_T(it, name):
                for j in range(2):
                    pe.wait_ge(ready["xn"], at(it, 6, 2 * XN[name] + j + 1))
                    turn(it, (name + "T", j), [xn[:, j, c * P:(c + 1) * P] for c in range(2)])

            with pe.Fori(0, PAIRS) as it:
                pe.wait_ge(enc_loaded, at(it, 16, 16))
                turn(it, ("encT",), [enc[:, j, :] for j in range(2)])
                pe.wait_ge(loaded["cross"], 16 * 3)
                wait_evacuated(pe, it, ("encT",))
                b = fill(it, ("ck",))
                done(mm(b[:, 0:2 * T], w_ckv[:, 0:C], both(encT[:]), start=True, stop=True), ("ck",))
                b = fill(it, ("cv",))
                for j in range(2):
                    i = mm(b[:, j * C:(j + 1) * C], encT[:, j, :], w_ckv[:, C:2 * C], start=True, stop=True)
                done(i, ("cv",))
                memory_projections(it, 0)
                for j in range(2):
                    pe.wait_ge(ready["xs"], at(it, 4, j + 1))
                    turn(it, ("xT", j), [xs[:, j, e, c * P:(c + 1) * P] for c in range(2) for e in range(2)])
                pe.wait_ge(loaded["self"], 16 * 4)
                for j in range(2):
                    wait_evacuated(pe, it, ("xT", j))
                    for name, lo, hi in (("qk", 0, 2 * H), ("v", 2 * H, 3 * H)):
                        b = fill(it, (name, j))
                        for k in range(4):
                            i = mm(b[:, 0:hi - lo], xT[:, k // 2, k % 2, j, :], w_qkv[:, k % 2, k // 2, lo:hi], start=k == 0,
                                   stop=k == 3)
                        done(i, (name, j))
                for j in range(2):
                    pe.wait_ge(ready["rot"], at(it, 2, j + 1))
                    turn(it, ("qkT", j), [rot[:, j, c * P:(c + 1) * P] for c in range(4)])
                wait_evacuated(pe, it, ("v", 1))
                wait_evacuated(pe, it, ("qkT", 1))
                attention(it, "self", score_self,
                          lambda g, j, h: v_self[:, j, h // 2 * 8 + 2 * g + h % 2, :], DS)
                for j in range(2):
                    wait_evacuated(pe, it, ("self", "pv", 6 + j))
                    turn(it, ("oT", j), [on[:, j, c * P:(c + 1) * P] for c in range(2)])
                for j in range(2):
                    wait_evacuated(pe, it, ("oT", j))
                    b = fill(it, ("dense", j))
                    for c in range(2):
                        i = mm(b[:, :], oT[:, j, c, :], w_dense[:, c, :], start=c == 0, stop=c == 1)
                    done(i, ("dense", j))
                norm_T(it, "ci")
                wait_evacuated(pe, it, ("ciT", 1))
                from_both(it, ("cq",), lambda c, o: w_cq[:, c, :], lambda c: both(nT[:, c]), [0], 2)
                wait_evacuated(pe, it, ("cq",))
                wait_evacuated(pe, it, ("ck",))
                attention(it, "cross", score_cross, lambda g, j, h: v_cross[:, j, 4 * g + h, :], DC)
                for j in range(2):
                    wait_evacuated(pe, it, ("cross", "pv", 6 + j))
                    turn(it, ("coT", j), [on[:, j, 0:P]])
                for j in range(2):
                    wait_evacuated(pe, it, ("coT", j))
                    b = fill(it, ("cdense", j))
                    done(mm(b[:, 0:H], oT[:, j, 0, :], w_cdense[:], start=True, stop=True), ("cdense", j))
                pe.wait_ge(loaded["kv2"], 16)
                for c in range(4):
                    from_both(it, ("k2", c), lambda _, o: w_kv2[:, o * P:(o + 1) * P], lambda _: both(encT[:]),
                              [2 * c, 2 * c + 1], 1)
                for j in range(2):
                    pe.wait_ge(ready["xs"], at(it, 4, 2 + j + 1))
                    turn(it, ("miT", j), [xs[:, j, e, c * P:(c + 1) * P] for c in range(2) for e in range(2)])
                pe.wait_ge(loaded["ffn"], 16 * 4)
                wait_evacuated(pe, it, ("miT", 0))
                wait_evacuated(pe, it, ("miT", 1))
                for i in range(FFC):
                    b = fill(it, ("ffn", i))
                    for u in range(2):
                        for k in range(4):
                            ins = mm(b[:, u * 2 * T:(u + 1) * 2 * T], w_gu[:, k % 2, k // 2, u, i * P:(i + 1) * P],
                                     both(xT[:, k // 2, k % 2]), start=k == 0, stop=k == 3)
                    done(ins, ("ffn", i))
                pe.wait_ge(loaded["down"], 16 * 4)
                for j in range(2):
                    b = fill(it, ("down", j))
                    for i in range(FFC):
                        wait_evacuated(pe, it, ("ffn", i))
                        ins = mm(b[:, :], hT[:, i, j, :], w_down[:, i, :], start=i == 0, stop=i == FFC - 1)
                    done(ins, ("down", j))
                memory(it, 0)
                for j in range(2):
                    for h in range(2):
                        b = fill(it, ("v2", j, h))
                        done(mm(b[:, :], encT[:, j, :], w_kv2[:, INNER + h * 512:INNER + (h + 1) * 512], start=True,
                                stop=True), ("v2", j, h))
                norm_T(it, "qn")
                pe.wait_ge(loaded["q2"], 16)
                wait_evacuated(pe, it, ("qnT", 0))
                wait_evacuated(pe, it, ("qnT", 1))
                for c in range(4):
                    from_both(it, ("q2", c), lambda k, o: w_q2[:, k, o * P:(o + 1) * P], lambda k: both(nT[:, k]),
                              [2 * c, 2 * c + 1], 2)
                wait_evacuated(pe, it, ("q2", 3))
                wait_evacuated(pe, it, ("k2", 3))
                wait_evacuated(pe, it, ("v2", 1, 1))
                pe.wait_ge(ready["mrow"], at(it, 1, 1))
                attention(it, "media", score_media,
                          lambda g, j, h: v_media[:, j, 2 * (g // 2 * 4 + h) + g % 2, :], DM)
                for h in range(2):
                    for j in range(2):
                        wait_evacuated(pe, it, ("media", "pv", (3 if h == 0 else 7) - 1 + j))
                        turn(it, ("o2T", j, h), [on[:, j, c * P:(c + 1) * P] for c in range(4 * h, 4 * h + 4)])
                pe.wait_ge(loaded["o2"], 16)
                for j in range(2):
                    wait_evacuated(pe, it, ("o2T", j, 0))
                    wait_evacuated(pe, it, ("o2T", j, 1))
                    b = fill(it, ("wo", j))
                    for c in range(MC):
                        i = mm(b[:, 0:H], o2T[:, j, c, :], w_o2[:, c, :], start=c == 0, stop=c == MC - 1)
                    done(i, ("wo", j))
                memory_projections(it, 1)
                norm_T(it, "hn")
                pe.wait_ge(loaded["ff2"], 16 * 2)
                wait_evacuated(pe, it, ("hnT", 0))
                wait_evacuated(pe, it, ("hnT", 1))
                for c in range(4):
                    from_both(it, ("ff2", c), lambda k, o: w_1[:, k, o * P:(o + 1) * P], lambda k: both(nT[:, k]),
                              [2 * c, 2 * c + 1], 2)
                for j in range(2):
                    b = fill(it, ("w2", j))
                    for c in range(MC):
                        if c % 2 == 0:
                            wait_evacuated(pe, it, ("ff2", c // 2))
                        i = mm(b[:, 0:H], h2T[:, c, j, :], w_2[:, c, :], start=c == 0, stop=c == MC - 1)
                    done(i, ("w2", j))
                wait_evacuated(pe, it, ("m1.mp",))
                memory(it, 1)


INS = ["x", "ctx_1024", "pos_1xS", "mask_BxS_ik0", "mask_BxS2_bk0"]
WEIGHTS = {
    0: ["ln_in_w", "ln_post_attn_w", "ln_post_cross_w", "v_qkv", "l_qkv", "v_dense", "l_dense", "cq_w", "ckv_w",
        "cdense_w", "v_gate", "v_up", "v_down", "l_gate", "l_up", "l_down"],
    1: ["W_mem", "W_gate", "b_gate", "norm_w"],
    2: ["ln_q_g", "ln_q_b", "Wq", "Wkv", "Wo", "attn_gate", "ln_ff_g", "ln_ff_b", "W1", "W2", "ff_gate"],
    3: ["W_mem", "W_gate", "b_gate", "norm_w"],
}


def kernel(**inputs):
    import concourse.bacc as bacc
    from concourse.bass_utils import run_bass_kernel_spmd

    nc = bacc.Bacc("TRN2", target_bir_lowering=False, num_devices=1)
    arrays, args = {}, {}
    given = {n: np.ascontiguousarray(inputs[n]) for n in INS}
    for b, names in WEIGHTS.items():
        for n in names:
            given[f"L{b}_xattn_{n}"] = np.ascontiguousarray(inputs[f"L{b}_xattn_{n}"])
    given["constants"] = constants()
    given["types_T"] = np.ascontiguousarray(given.pop("mask_BxS_ik0").T)
    given["columns"] = np.ascontiguousarray(np.concatenate(
        [given.pop(n).reshape(2, P).T for n in (
            "L0_xattn_ln_in_w", "L0_xattn_ln_post_cross_w", "L0_xattn_ln_post_attn_w", "L2_xattn_ln_q_g",
            "L2_xattn_ln_q_b", "L2_xattn_ln_ff_g", "L2_xattn_ln_ff_b")], axis=1))
    for n in ("L1_xattn_W_mem", "L1_xattn_W_gate", "L3_xattn_W_mem", "L3_xattn_W_gate"):
        given[n] = np.ascontiguousarray(given[n].T)
    for name, a in given.items():
        arrays[f"in_{name}"] = a
        dtype = U8 if a.dtype == bool else mybir.dt.from_np(a.dtype)
        args[name] = nc.dram_tensor(f"in_{name}", a.shape, dtype, kind="ExternalInput").ap()
    out = nc.dram_tensor("out", (B, T, H), F32, kind="ExternalOutput").ap()
    build(nc, args, out)
    r = run_bass_kernel_spmd(nc, [arrays], core_ids=[0])
    return r.results[0]["out"]
```

```python
from contextlib import ExitStack

import concourse.bass as bass
from concourse import mybir
import numpy as np

F32 = mybir.dt.float32
BF16 = mybir.dt.bfloat16
F16 = mybir.dt.float16
F32R = mybir.dt.float32r
I32 = mybir.dt.int32
U8 = mybir.dt.uint8
ALU = mybir.AluOpType
ACT = mybir.ActivationFunctionType
AX = mybir.AxisListType

B, T, H, C = 8, 128, 256, 128
P = 128
NH = 16
DS, DC, DM = 16, 8, 64
FF = 688
FFC = -(-FF // P)
FFP = FFC * P
FFL = FF - (FFC - 1) * P
INNER = NH * DM
MC = INNER // P
UNITS = 4
LAGS = {"S": 0, "T": 1, "V": 2, "N": 3}
POOL_SETUP, SMALL = 12, 6
LINKS_A, LINKS_B = 26, 10
NEG = -1e30

C_ID, C_CAUSAL, C_EO, C_M4, C_COS, C_SIN, C_IOTA, C_END = np.cumsum([0, P, P, 2, 4, DS, DS, 1]).tolist()


def constants():
    c = np.zeros((P, C_END), np.float32)
    p = np.arange(P)
    c[:, C_ID:C_ID + P] = np.eye(P)
    c[:, C_CAUSAL:C_CAUSAL + P] = np.where(p[None, :] > p[:, None], NEG, 0)
    c[:, C_EO:C_EO + 2] = (p[:, None] % 32) // DS == np.arange(2)
    c[:, C_M4:C_M4 + 4] = (p[:, None] % 32) // DC == np.arange(4)
    inv = np.float32(1.0) / np.float32(10000.0) ** (np.arange(0, DS, 2, dtype=np.float32) / np.float32(DS))
    f = np.outer(np.arange(T, dtype=np.float32), inv).astype(np.float32)
    c[:, C_COS:C_COS + DS] = np.cos(np.concatenate([f, f], 1))
    c[:, C_SIN:C_SIN + DS] = np.sin(np.concatenate([-f, f], 1))
    c[:, C_IOTA] = p
    return c


def attention_steps(a):
    fills = {"S": ("S", "score"), "T": ("T", "pT"), "V": ("M", "pv")}
    return [(f"{a}.{stage}{n - lag}", [(fills[stage][0], f"{a}.{fills[stage][1]}.{n - lag}")] if stage in fills else [])
            for n in range(UNITS + LAGS["N"]) for stage, lag in LAGS.items() if 0 <= n - lag < UNITS]


def norm_steps(n):
    return [(f"{n}.q", []), (f"{n}.n", []), (f"{n}.T", [("T", f"{n}T")])]


def memory_steps(m):
    return [(f"{m}.mp", [("M", f"{m}.mpT"), ("M", f"{m}.mp")]), (f"{m}.x", [("T", f"{m}.xT")]), (f"{m}.s", [("S", f"{m}.score")]),
            (f"{m}.e", []), (f"{m}.p", [("T", f"{m}.pT")]), (f"{m}.c", [("M", f"{m}.mc")]),
            (f"{m}.t", [("T", f"{m}.mcT")]), (f"{m}.g", [("M", f"{m}.gate")]), (f"{m}.f", []), (f"{m}.q", []), (f"{m}.n", [])]


HALF_A = [
    ("enc.T", [("T", "encT")]),
    ("enc.k", [("M", "ckv")]),
    ("ckT", [("T", "ckT")]),
    *norm_steps("in"),
    ("qkv", [("M", "qk"), ("M", "v")]),
    ("rope.r", []),
    ("rope.T", [("T", "qkT")]),
    *attention_steps("self"),
    ("oT", [("T", "oT")]),
    ("dense", [("M", "dense")]),
    *norm_steps("ci"),
    ("cq", [("M", "cq")]),
    ("cqT", [("T", "cqT")]),
    *attention_steps("cross"),
    ("coT", [("T", "coT")]),
    ("cdense", [("M", "cdense")]),
    *norm_steps("mi"),
    *[(f"ffn.{i}", [("M", f"ffn.{i}")]) for i in range(FFC // 2)],
    ("down", [("M", "down")]),
]
HALF_B = [
    ("encb.T", [("T", "encbT")]),
    ("encb.k", [("M", "k2.0"), ("M", "k2.1")]),
    ("v2", [("M", "v2.0"), ("M", "v2.1")]),
    *memory_steps("m0"),
    *norm_steps("qn"),
    ("q2.0", [("M", "q2.0")]),
    ("q2.1", [("M", "q2.1")]),
    *attention_steps("media"),
    ("o2T.0", [("T", "o2T.0")]),
    ("o2T.1", [("T", "o2T.1")]),
    ("wo", [("M", "wo")]),
    *memory_steps("m1")[:1],
    *norm_steps("hn"),
    ("ff2.0", [("M", "ff2.0")]),
    ("ff2.1", [("M", "ff2.1")]),
    ("w2", [("M", "w2")]),
    *memory_steps("m1")[1:],
]


def reordered(half, names, before):
    steps = dict(half)
    order = [n for n in steps if n not in names]
    k = order.index(before)
    return [(n, steps[n]) for n in order[:k] + names + order[k:]]


ALONE_A = reordered(reordered(HALF_A, ["enc.T", "enc.k"], "rope.r"), ["ckT"], "self.S0")
ALONE_B = reordered(HALF_B, ["encb.k", "v2"], "m0.e")


ORDER = ("ABABAAABBABBBAABABBAABBABABBAAABBAAAABAAABAAABBABABABBAB"
         "BABBBABBABBBBABAABBBAAABBAAAABAAABAAAAAABABBBABABABBBBAB")


def merged(order):
    rest = {"A": iter(HALF_A), "B": iter(HALF_B)}
    return [next(rest[half]) for half in order]


class Phase:
    RINGS = {"T": (0, 1), "S": (2, 3), "M": (4, 5, 6, 7)}

    def __init__(self, steps, base):
        self.steps, self.base, self.of = steps, dict(base), {}
        self.per = {b: 0 for r in self.RINGS.values() for b in r}
        used = {k: 0 for k in self.RINGS}
        for _, fills in steps:
            for ring, name in fills:
                bank = self.RINGS[ring][used[ring] % len(self.RINGS[ring])]
                used[ring] += 1
                self.of[name] = (bank, self.per[bank])
                self.per[bank] += 1

    def after(self, passes):
        return {b: self.base[b] + passes * n for b, n in self.per.items()}


def build(nc, t, out):
    first = Phase(ALONE_A, {b: 0 for b in range(8)})
    middle = Phase(merged(ORDER), first.after(1))
    last = Phase(ALONE_B, middle.after(B - 1))
    with ExitStack() as ctx:
        def sb(name, shape, dt=F32):
            return ctx.enter_context(nc.sbuf_tensor(name, shape, dt))

        def sem(name):
            return ctx.enter_context(nc.semaphore(name))

        cst = sb("cst", [P, C_END])
        ident = cst[:, C_ID:C_ID + P]
        identb = sb("identb", [P, P], BF16)
        causal = sb("causal", [P, 4, P], BF16)
        onesb = sb("onesb", [3, P], BF16)
        minus_half = sb("minus_half", [P, 1])
        w_qkv = sb("w_qkv", [P, 2, 2, 3 * H])
        w_dense = sb("w_dense", [P, 2, 2 * H])
        w_cq = sb("w_cq", [P, 2, C])
        w_ckv = sb("w_ckv", [P, 2 * C])
        w_cdense = sb("w_cdense", [P, H])
        w_gu = sb("w_gu", [P, 2, 2, 2, FFP])
        w_down = sb("w_down", [P, FFC, 2 * H])
        w_memT = sb("w_memT", [P, 2, H])
        w_gateT = sb("w_gateT", [P, 2, 4, H])
        b_gate = sb("b_gate", [3, 2, H])
        b_part = sb("b_part", [3, 2, H], BF16)
        b_parts = sb("b_parts", [3, 2, H], BF16)
        norm_w = sb("norm_w", [P, 2, H])
        w_q2 = sb("w_q2", [P, 2, INNER])
        w_kv2 = sb("w_kv2", [P, 2 * INNER])
        w_o2 = sb("w_o2", [P, MC, H])
        w_1 = sb("w_1", [P, 2, INNER])
        w_2 = sb("w_2", [P, MC, H])
        cols = sb("cols", [P, 7, 2])
        LN_IN, LN_CROSS, LN_ATTN, Q_G, Q_B, FF_G, FF_B = range(7)
        gates = sb("gates", [P, 2])
        tgates = sb("tgates", [P, 2])
        rope = sb("rope", [P, 2 * DS])
        tt_i = sb("tt_i", [P, 2, B], I32)
        tt_f = sb("tt_f", [P, 2, B])
        vm_all = sb("vm_all", [P, 2, B])

        x_in = sb("x_in", [P, H])
        enc = sb("enc", [P, C])
        encT = sb("encT", [P, T])
        vm = sb("vm", [P, 2])
        work_1, work_2 = sb("work_1", [P, 2 * H]), sb("work_2", [P, 2 * H])
        xs = work_1[:].rearrange("p (e n) -> p e n", e=2)
        xT = sb("xT", [P, 2, 2, T])
        rot, rot2 = work_1, work_2
        qT = sb("qT", [P, 2, T])
        keo = sb("keo", [P, 2, 2, T])
        v_self = sb("v_self", [P, NH, 3, DS + 1], BF16)
        v_self_rest = sb("v_self_rest", [P, NH, DS])
        cq_parts = sb("cq_parts", [P, UNITS, 3, 32])
        ck_parts = sb("ck_parts", [P, UNITS, 3, 32])
        pos_i = ck_parts[:].rearrange("p u s d -> p (u s d)")[:, 0:T].bitcast(I32)
        pos_f = work_2[:].rearrange("p (k t) -> p k t", k=4)[:, 0:2]
        cqT = sb("cqT", [96, UNITS, T])
        ckm = sb("ckm", [96, UNITS, 4, T])
        v_cross = sb("v_cross", [P, NH, 3, DC + 1], BF16)
        v_cross_rest = sb("v_cross_rest", [P, NH, DC])
        on_a = sb("on_a", [P, H])
        oT = sb("oT", [P, 2, T])
        x1 = sb("x1", [P, H])
        x2 = sb("x2", [P, H])
        x3 = sb("x3", [P, H])
        xn_a = on_a
        nT_a = sb("nT_a", [P, 2, T])
        th, tg = (x[:].rearrange("p (k t) -> p k t", k=2) for x in (work_2, work_1))
        hT = sb("hT", [P, FFC, T])
        junk_a = sb("junk_a", [P, H])

        encb = sb("encb", [P, C])
        encbT = sb("encbT", [P, T])
        mm_u8 = sb("mm_u8", [1, T], U8)
        mrow = sb("mrow", [1, 4, T], BF16)
        mpT = sb("mpT", [P, 2, T])
        mp = sb("mp", [P, H])
        lT = sb("lT", [P, 4, T])
        mmx = sb("mmx", [P, 4])
        mpr = sb("mpr", [P, T])
        mpr_T = sb("mpr_T", [P, T])
        mc = sb("mc", [P, H])
        gth = sb("gth", [P, H])
        fus = sb("fus", [P, H])
        junk_b = sb("junk_b", [P, H])
        bns = sb("bns", [P, 6])
        x4 = sb("x4", [P, H])
        x5 = sb("x5", [P, H])
        x6 = x4
        y = sb("y", [P, H])
        xn_b = gth
        nT_b = sb("nT_b", [P, 2, T])
        qT2 = sb("qT2", [P, MC, T])
        kT2 = sb("kT2", [P, MC, T])
        v_media = sb("v_media", [P, NH, 3, DM + 1], BF16)
        on_b = sb("on_b", [P, INNER])
        v_media_rest = on_b[:].rearrange("p (h d) -> p h d", h=NH)
        o2T = sb("o2T", [P, MC, T])
        h2T = qT2

        var = sb("var", [P, 7, 2])
        vare = sb("vare", [P, 7])
        rstd = sb("rstd", [P, 7])
        mx = sb("mx", [P, 2, 3, 4])
        rec = sb("rec", [P, 2, 2, 4])
        pr = sb("pr", [P, 2, 2, 4 * P])
        pT_hi = sb("pT_hi", [P, 2, 2, 4 * P], F16)
        pT_lo = sb("pT_lo", [P, 2, 2, 4 * P], F16)
        sums = sb("sums", [P, 2, 4, DS + 1])
        bank = [ctx.enter_context(nc.psum_tensor(f"bank{k}", [P, 512], F32)) for k in range(8)]

        filled = [sem(f"filled{k}") for k in range(8)]
        drained = [sem(f"drained{k}") for k in range(8)]
        loaded = {n: sem(f"loaded_{n}") for n in ("const", "pos", "types", "cols", "small", "self", "dense", "ckv", "cross",
                                                  "kv2", "m", "ffn", "down", "q2", "o2", "ff2")}
        x_loaded, enc_loaded, encb_loaded, mask_loaded, y_stored = (
            sem(n) for n in ("x_loaded", "enc_loaded", "encb_loaded", "mask_loaded", "y_stored"))
        pads_zero = sem("pads_zero")
        pool_setup, dve_setup, pe_setup, act_setup = (sem(f"{n}_setup") for n in ("pool", "dve", "pe", "act"))
        dve_chain = sem("dve_chain")
        pool_chain, pool_parts = sem("pool_chain"), sem("pool_parts")
        passed_pool, passed_dve, passed_sp = sem("passed_pool"), sem("passed_dve"), sem("passed_sp")
        var_ready = [sem(f"var_ready{n}") for n in range(7)]
        rstd_ready = [sem(f"rstd_ready{n}") for n in range(7)]
        ready = {n: sem(f"{n}_ready") for n in ("masks", "onehot", "rope", "mrow", "xs", "rot", "maxima_a", "maxima_b", "hi_a", "hi_b",
                                                "v_hi_a", "v_hi_b", "cq_hi", "ckm_act", "bias", "v_media", "xn_a",
                                                "xn_b", "tanh", "mneg", "fused", "x4", "y")}
        block = ctx.enter_context(nc.Block())

        ATT = {"self": (0, 0, DS), "cross": (0, 1, DC), "media": (1, 0, DM)}
        MAXIMA, HIGH = ("maxima_a", "maxima_b"), ("hi_a", "hi_b")

        def at(row, per, k):
            return row * per + k

        class Place:

            def __init__(self, phase, passes, row_a, row_b):
                self.phase, self.passes, self.a, self.b = phase, passes, row_a, row_b

            def count(self, name, more):
                b, k = self.phase.of[name]
                return self.passes * self.phase.per[b] + (self.phase.base[b] + k + more)

            def drained(self, evacuated, filling=()):
                counts = {}
                for names, more in ((evacuated, 2), (filling, 1)):
                    for name in names:
                        b, k = self.phase.of[name]
                        counts[b] = max(counts.get(b, 0), self.phase.base[b] + k + more)
                return [(b, self.passes * self.phase.per[b] + n) for b, n in counts.items()]

        def run(eng, step):
            for name, _ in first.steps:
                step(Place(first, 0, 0, None), name)
            with eng.Fori(0, B - 1) as i:
                for name, _ in middle.steps:
                    step(Place(middle, i, i + 1, i), name)
            for name, _ in last.steps:
                step(Place(last, 0, None, B - 1), name)

        def wait_filled(eng, w, name):
            b = w.phase.of[name][0]
            eng.wait_ge(filled[b], w.count(name, 1))
            return bank[b]

        def wait_evacuated(eng, w, name):
            eng.wait_ge(drained[w.phase.of[name][0]], w.count(name, 2))

        def gone(w, name):
            return drained[w.phase.of[name][0]]

        def chunks(a):
            return a.rearrange("(c p) n -> p c n", p=P)

        NORMS = [(1 / H, 1e-6)] * 4 + [(1.0, 1e-5)] * 2 + [(1 / H, 1e-6)]
        N_IN, N_CROSS, N_ATTN, N_M0, N_Q, N_FF, N_M1 = range(7)
        BLOCKS = {"m0": (0, x3, x4, N_M0, "x4"), "m1": (1, x6, y, N_M1, "y")}

        @block.sync
        def _(sp):
            def get(group, to, source):
                sp.dma_start(to, source).then_inc(loaded[group], 16)

            def load_enc(row):
                sp.dma_start(enc[:], t["ctx_1024"][bass.ds(row, 1)].rearrange("b t n -> (b t) n")).then_inc(enc_loaded, 16)

            def load_x(row):
                sp.dma_start(x_in[:], t["x"][bass.ds(row, 1)].rearrange("b t n -> (b t) n")).then_inc(x_loaded, 16)

            def load_b(row):
                sp.dma_start(encb[:], t["ctx_1024"][bass.ds(row, 1)].rearrange("b t n -> (b t) n")).then_inc(encb_loaded, 16)
                sp.dma_start(mm_u8[:], t["mask_BxS2_bk0"][bass.ds(row, 1), :]).then_inc(mask_loaded, 16)

            load_x(0)
            get("const", cst[:], t["constants"])
            load_enc(0)
            get("types", tt_i[:, 0, :], t["types_T"])
            sp.wait_ge(pool_setup, 1)
            get("types", tt_i[0:T - 1, 1, :], t["types_T"][1:T, :])
            get("cols", cols[:].rearrange("p k c -> p (k c)"), t["columns"])
            get("pos", pos_i, t["pos_1xS"][0].partition_broadcast(P))
            get("ckv", w_ckv[:], t["L0_xattn_ckv_w"])
            get("dense", w_dense[:, :, 0:H], chunks(t["L0_xattn_v_dense"]))
            get("dense", w_dense[:, :, H:2 * H], chunks(t["L0_xattn_l_dense"]))
            get("cross", w_cq[:], chunks(t["L0_xattn_cq_w"]))
            get("cross", w_cdense[:], t["L0_xattn_cdense_w"])
            sp.wait_ge(pads_zero, 2)
            for e, n in enumerate("vl"):
                for k, g in enumerate(("gate", "up")):
                    get("ffn", w_gu[:, e, :, k, 0:FF], chunks(t[f"L0_xattn_{n}_{g}"]))
            for e, n in enumerate("vl"):
                w = t[f"L0_xattn_{n}_down"]
                get("down", w_down[:, 0:FFC - 1, e * H:(e + 1) * H], chunks(w[0:(FFC - 1) * P, :]))
                get("down", w_down[0:FFL, FFC - 1, e * H:(e + 1) * H], w[(FFC - 1) * P:FF, :])
            load_b(0)
            get("kv2", w_kv2[:], t["L2_xattn_Wkv"])
            for k, b in enumerate((1, 3)):
                get("m", w_memT[:, k, :], t[f"L{b}_xattn_W_mem"])
                get("m", w_gateT[:, k], chunks(t[f"L{b}_xattn_W_gate"]))
            get("small", gates[:, 0:1], t["L2_xattn_attn_gate"].partition_broadcast(P))
            get("small", gates[:, 1:2], t["L2_xattn_ff_gate"].partition_broadcast(P))
            for k, b in enumerate((1, 3)):
                get("small", b_gate[:, k, :], t[f"L{b}_xattn_b_gate"].partition_broadcast(3))
                get("small", norm_w[:, k, :], t[f"L{b}_xattn_norm_w"].partition_broadcast(P))
            get("q2", w_q2[:], chunks(t["L2_xattn_Wq"]))
            get("o2", w_o2[:], chunks(t["L2_xattn_Wo"]))
            get("ff2", w_1[:], chunks(t["L2_xattn_W1"]))
            get("ff2", w_2[:], chunks(t["L2_xattn_W2"]))

            def passed():
                sp.sem_inc(passed_sp, 1)

            def next_row_a(w, row):
                wait_filled(sp, w, "encT")
                passed()
                load_enc(row)
                wait_evacuated(sp, w, "dense")
                passed()
                load_x(row)

            def next_row_b(w, row):
                wait_filled(sp, w, "encbT")
                passed()
                sp.wait_ge(ready["mrow"], at(w.b, 1, 1))
                passed()
                load_b(row)

            def store(w):
                sp.wait_ge(ready["y"], at(w.b, 1, 1))
                passed()
                sp.dma_start(out[bass.ds(w.b, 1)].rearrange("b t n -> (b t) n"), y[:]).then_inc(y_stored, 16)

            next_row_a(Place(first, 0, 0, None), 1)
            with sp.Fori(0, B - 2) as i:
                w = Place(middle, i, i + 1, i)
                next_row_b(w, i + 1)
                next_row_a(w, i + 2)
                store(w)
            w = Place(middle, B - 2, B - 1, B - 2)
            next_row_b(w, B - 1)
            store(w)
            store(Place(last, 0, None, B - 1))
            sp.wait_ge(y_stored, 16 * B + 16)

        @block.gpsimd
        def _(pool):
            nc.gpsimd.memset(tt_i[:, 1, :], 0).then_inc(pool_setup, 1)
            nc.gpsimd.memset(onesb[:], 1.0).then_inc(pool_setup, 1)
            nc.gpsimd.memset(minus_half[:], -0.5).then_inc(pool_setup, 1)
            for part, one in enumerate((1.0, 0.0, 0.0)):
                for v, width in ((v_self, DS), (v_cross, DC), (v_media, DM)):
                    nc.gpsimd.memset(v[:, :, part, width:width + 1], one).then_inc(pool_setup, 1)
            nc.gpsimd.memset(w_gu[:, :, :, :, FF:FFP].rearrange("p e c k n -> p (e c k) n"), 0.0).then_inc(pads_zero, 1)
            nc.gpsimd.memset(w_down[:, FFC - 1, :], 0.0).then_inc(pads_zero, 1)
            pool.wait_ge(pool_setup, POOL_SETUP)

            def inverse_root(w, n):
                scale, eps = NORMS[n]
                row = w.a if n < N_M0 else w.b
                turns[0] += 1
                pool.wait_ge(var_ready[n], at(row, 1, 1))
                pool.sem_inc(passed_pool, 1)
                nc.gpsimd.tensor_scalar(vare[:, n:n + 1], var[:, n, 1:2], scale, eps, ALU.mult, ALU.add)\
                    .then_inc(pool_chain, 1)
                pool.wait_ge(pool_chain, w.passes * len(NORMS) + turns[0])
                nc.gpsimd.tensor_tensor(rstd[:, n:n + 1], vare[:, n:n + 1], minus_half[:], ALU.pow)\
                    .then_inc(rstd_ready[n], 1)

            turns = [0]
            norm_of = {"in.q": N_IN, "ci.q": N_CROSS, "mi.q": N_ATTN, "m0.q": N_M0, "qn.q": N_Q, "hn.q": N_FF, "m1.q": N_M1}

            def step(w, name):
                if w.phase is last and w.phase.steps[0][0] == name:
                    turns[0] += (B - 2) * len(NORMS)
                if name == "v2":
                    for h in range(2):
                        v, rest = v_media[:, 8 * h:8 * h + 8, :, 0:DM], v_media_rest[:, 8 * h:8 * h + 8, :]
                        wait_evacuated(pool, w, f"v2.{h}")
                        pool.sem_inc(passed_pool, 1)
                        nc.gpsimd.tensor_copy(v[:, :, 1, :], rest).then_inc(pool_parts, 1)
                        pool.wait_ge(pool_parts, at(w.b, 2, h + 1))
                        nc.gpsimd.tensor_tensor(v[:, :, 2, :], rest, v[:, :, 1, :], ALU.subtract)\
                            .then_inc(ready["v_media"], 1)
                if name in norm_of:
                    inverse_root(w, norm_of[name])

            run(pool, step)

        @block.scalar
        def _(act):
            copy, exp, tanh = ACT.Copy, ACT.Exp, ACT.Tanh
            act.dma_start(w_qkv[:, 0], chunks(t["L0_xattn_v_qkv"])).then_inc(loaded["self"], 16)
            act.dma_start(w_qkv[:, 1], chunks(t["L0_xattn_l_qkv"])).then_inc(loaded["self"], 16)

            def evacuate(w, name, to, of=lambda b: b[:, :], func=copy, **kw):
                b = wait_filled(act, w, name)
                nc.scalar.activation(to, of(b), func, **kw).then_inc(gone(w, name), 1)

            def first_part(w, name, to, of, heads):
                b = wait_filled(act, w, name)
                nc.scalar.activation(to, of(b).rearrange("p (h d) -> p h d", h=heads), copy).then_inc(ready["v_hi_b" if name[:2] == "v2" else "v_hi_a"], 1)

            def high_twice(x, to, scale):
                return nc.scalar.activation(to.bitcast(F32R), x.rearrange("p (u d) -> p u d", u=UNITS).unsqueeze(2)
                                            .broadcast_to([P, UNITS, 2, 32]), copy, scale=scale)

            def squares(n, x, junk):
                nc.scalar.activation(junk[:], x[:], ACT.Square, accum_out=var[:, n, 1:2]).then_inc(var_ready[n], 1)

            def attention(w, a, stage, n):
                half, turn, _ = ATT[a]
                if stage == "T":
                    b = wait_filled(act, w, f"{a}.pT.{n}")
                    if n >= 2:
                        wait_filled(act, w, f"{a}.pv.{n - 2}")
                    nc.scalar.copy(pT_hi[:, half, n % 2, :], b[:, :]).then_inc(ready[HIGH[half]], 1)
                if stage == "S":
                    b = bank[w.phase.of[f"{a}.score.{n}"][0]]
                    row, per = (w.a, 2 * UNITS) if half == 0 else (w.b, UNITS)
                    act.wait_ge(ready[MAXIMA[half]], at(row, per, turn * UNITS + n + 1))
                    for h in range(4):
                        i = nc.scalar.activation(pr[:, half, n % 2, h * P:(h + 1) * P], b[:, h * P:(h + 1) * P], exp,
                                                 bias=mx[:, half, n % 3, h:h + 1])
                    i.then_inc(gone(w, f"{a}.score.{n}"), 1)

            def scaled_T(w, name, k, to, shift=None):
                b = wait_filled(act, w, name)
                n = 2 * T if name in ("inT", "miT") else T
                for c in range(2):
                    kw = {"bias": cols[:, shift, c:c + 1]} if shift is not None else {}
                    i = nc.scalar.activation(to[:, c], b[:, c * n:(c + 1) * n], ACT.Identity if kw else copy,
                                             scale=cols[:, k, c:c + 1], **kw)
                i.then_inc(gone(w, name), 1)

            def memory(w, m, what):
                k, src, dst, norm, _ = BLOCKS[m]
                if what == "mp":
                    evacuate(w, f"{m}.mpT", mpT[:].rearrange("p c t -> p (c t)"), lambda b: b[:, 0:2 * T], scale=H ** -0.5)
                if what == "x":
                    evacuate(w, f"{m}.xT", lT[:, 0:2, :].rearrange("p c t -> p (c t)"), lambda b: b[:, 0:2 * T])
                if what == "e":
                    b = wait_filled(act, w, f"{m}.score")
                    act.wait_ge(ready["mneg"], at(w.b, 2, k + 1))
                    nc.scalar.activation(mpr[:], b[:, 0:T], exp, bias=mmx[:, 1:2],
                                         accum_out=mmx[:, 2:3]).then_inc(gone(w, f"{m}.score"), 1)
                if what == "p":
                    evacuate(w, f"{m}.pT", mpr_T[:], lambda b: b[:, 0:T])
                if what == "t":
                    evacuate(w, f"{m}.mcT", lT[:, 2:4, :].rearrange("p c t -> p (c t)"), lambda b: b[:, 0:2 * T])
                if what == "g":
                    evacuate(w, f"{m}.gate", gth[:], lambda b: b[:, 0:H], tanh, scale=0.5)
                if what == "q":
                    act.wait_ge(ready["fused"], at(w.b, 2, k + 1))
                    squares(norm, fus, junk_b)

            def step(w, name):
                what, _, n = name.partition(".")
                if what in ATT:
                    attention(w, what, n[0], int(n[1]))
                elif name == "o2T.0":
                    evacuate(w, "o2T.0", o2T[:, 0:4, :].rearrange("p c t -> p (c t)"))
                elif what in BLOCKS:
                    memory(w, what, n)
                elif name == "enc.T":
                    evacuate(w, "encT", encT[:], lambda b: b[:, 0:T])
                elif name == "enc.k":
                    b = wait_filled(act, w, "ckv")
                    high_twice(b[:, 0:C], ck_parts[:, :, 0:3:2, :], 1.0)
                    first_part(w, "ckv", v_cross[:, :, 0, 0:DC], lambda b: b[:, C:2 * C], NH)
                elif name == "ckT":
                    b = wait_filled(act, w, "ckT")
                    for h in range(2):
                        i = nc.scalar.activation(ckm[:, :, h, :].bitcast(F32R), b[0:96, :].rearrange("p (u t) -> p u t", u=4),
                                                 copy, scale=cst[0:96, C_M4 + h:C_M4 + h + 1])
                    i.then_inc(ready["ckm_act"], 1)
                elif name == "in.q":
                    act.wait_ge(x_loaded, at(w.a, 16, 16))
                    squares(N_IN, x_in, junk_a)
                    if w.phase is first:
                        act.wait_ge(loaded["cols"], 16)
                elif name == "in.T":
                    scaled_T(w, "inT", LN_IN, xT[:].rearrange("p c e t -> p c (e t)"))
                elif name == "rope.r":
                    first_part(w, "v", v_self[:, :, 0, 0:DS], lambda b: b[:, 0:H], NH)
                elif name == "rope.T":
                    b = wait_filled(act, w, "qkT")
                    nc.scalar.activation(qT[:].rearrange("p g t -> p (g t)"), b[:, 0:2 * T], copy, scale=DS ** -0.5)
                    for e in range(2):
                        i = nc.scalar.activation(keo[:, :, e, :], b[:, 2 * T:].rearrange("p (g t) -> p g t", g=2), copy,
                                                 scale=cst[:, C_EO + e:C_EO + e + 1])
                    i.then_inc(gone(w, "qkT"), 1)
                elif name == "oT":
                    evacuate(w, "oT", oT[:].rearrange("p c t -> p (c t)"), lambda b: b[:, 0:2 * T])
                elif name == "ci.q":
                    wait_evacuated(act, w, "dense")
                    squares(N_CROSS, x1, junk_a)
                elif name == "ci.T":
                    scaled_T(w, "ciT", LN_CROSS, nT_a)
                elif name == "cq":
                    b = wait_filled(act, w, "cq")
                    high_twice(b[:, 0:C], cq_parts[:, :, 0:2, :], DC ** -0.5).then_inc(ready["cq_hi"], 1)
                elif name == "cqT":
                    evacuate(w, "cqT", cqT[:].rearrange("p u t -> p (u t)").bitcast(F32R), lambda b: b[0:96, :])
                elif name == "coT":
                    evacuate(w, "coT", oT[:, 0, :], lambda b: b[:, 0:T])
                elif name == "mi.q":
                    wait_evacuated(act, w, "cdense")
                    squares(N_ATTN, x2, junk_a)
                elif name == "mi.T":
                    scaled_T(w, "miT", LN_ATTN, xT[:].rearrange("p c e t -> p c (e t)"))
                elif what == "ffn":
                    i = int(n)
                    b = wait_filled(act, w, name)
                    if i >= 2:
                        wait_evacuated(act, w, f"ffn.{i - 2}")
                    nc.scalar.activation(th[:, i % 2, :], b[:, 0:2 * T], tanh, scale=0.5).then_inc(ready["tanh"], 1)
                elif name == "encb.T":
                    evacuate(w, "encbT", encbT[:], lambda b: b[:, 0:T])
                elif name == "v2":
                    for h in range(2):
                        first_part(w, f"v2.{h}", v_media[:, h * 8:h * 8 + 8, 0, 0:DM], lambda b: b[:, :], 8)
                elif name == "qn.T":
                    scaled_T(w, "qnT", Q_G, nT_b, Q_B)
                elif what == "q2":
                    c = int(n)
                    evacuate(w, name, qT2[:, 4 * c:4 * c + 4].rearrange("p c t -> p (c t)"), scale=DM ** -0.5)
                elif name == "hn.T":
                    scaled_T(w, "hnT", FF_G, nT_b, FF_B)
                elif what == "ff2":
                    c = int(n)
                    evacuate(w, name, h2T[:, 4 * c:4 * c + 4].rearrange("p c t -> p (c t)"), func=ACT.Gelu)
                if w.phase is first and name == "down":
                    act.wait_ge(loaded["small"], 16 * SMALL)
                    nc.scalar.activation(tgates[:], gates[:], tanh).then_inc(act_setup, 1)

            run(act, step)

        @block.vector
        def _(dve):
            chained = [0]

            def link(w, ins):
                chained[0] += 1
                ins.then_inc(dve_chain, 1)
                dve.wait_ge(dve_chain, w.passes * (LINKS_A + LINKS_B) + chained[0])

            steps = [0]

            def setup(ins):
                steps[0] += 1
                ins.then_inc(dve_setup, 1)
                dve.wait_ge(dve_setup, steps[0])

            for k, a in zip((0, 1, 2, 3, 4, 6, 7), (mx[:, 0, 0], mx[:, 0, 1], mx[:, 0, 2], rec[:, 0, 0], rec[:, 0, 1],
                                                    mmx[:, 0:2], mmx[:, 2:4])):
                nc.vector.memset(a, 0.0).then_inc(drained[k], 1)
            nc.vector.memset(y[:], 0.0).then_inc(y_stored, 16)
            dve.wait_ge(loaded["types"], 32)
            setup(nc.vector.tensor_scalar(tt_f[:], tt_i[:], 1.0, None, ALU.is_equal))
            setup(nc.vector.tensor_tensor(vm_all[:, 0, :], tt_f[:, 0, :], tt_f[:, 1, :], ALU.mult))
            setup(nc.vector.tensor_scalar(vm_all[:, 1, :], vm_all[:, 0, :], -1.0, 1.0, ALU.mult, ALU.add))
            dve.wait_ge(loaded["const"], 16)
            nc.vector.tensor_copy(identb[:], ident).then_inc(ready["masks"], 1)
            nc.vector.tensor_copy(causal[:], cst[:, C_CAUSAL:C_CAUSAL + P].unsqueeze(1).broadcast_to([P, 4, P]))\
                .then_inc(ready["masks"], 1)

            def positions():
                dve.wait_ge(loaded["pos"], 16)
                pf, pg = pos_f[:, 0, :], pos_f[:, 1, :]
                setup(nc.vector.tensor_copy(pf, pos_i))
                setup(nc.vector.tensor_scalar(pg, pf, 0.0, float(T), ALU.is_lt, ALU.mult))
                setup(nc.vector.tensor_tensor(pf, pf, pg, ALU.add))
                setup(nc.vector.tensor_scalar(pf, pf, 0.0, float(T - 1), ALU.max, ALU.min))
                nc.vector.tensor_scalar(pg, pf, cst[:, C_IOTA:C_IOTA + 1], None, ALU.is_equal).then_inc(ready["onehot"], 1)
                dve.wait_ge(pe_setup, 1)
                setup(nc.vector.tensor_copy(rope[:], bank[5][:, 0:2 * DS]))
                nc.vector.memset(bns[:], 0.0).then_inc(drained[5], 1)

            positions()

            def bias_parts():
                dve.wait_ge(loaded["small"], 16 * SMALL)
                for k in range(3):
                    mine = cst[0:3, C_ID + k:C_ID + k + 1]
                    setup(nc.vector.tensor_copy(b_part[:], b_gate[:]))
                    if k == 0:
                        setup(nc.vector.tensor_scalar(b_parts[:], b_part[:], mine, None, ALU.mult))
                    else:
                        setup(nc.vector.scalar_tensor_tensor(b_parts[:], b_part[:], mine, b_parts[:], ALU.mult, ALU.add))
                    i = nc.vector.tensor_tensor(b_gate[:], b_gate[:], b_part[:], ALU.subtract)
                    if k < 2:
                        setup(i)
                i.then_inc(ready["bias"], 1)

            def attention(w, a, stage, n):
                half, turn, width = ATT[a]
                if stage == "S":
                    s = wait_filled(dve, w, f"{a}.score.{n}")[:, :].rearrange("p (h k) -> p h k", h=4)
                    nc.vector.tensor_reduce(mx[:, half, n % 3, :], s, AX.X, ALU.max, negate=True)\
                        .then_inc(ready[MAXIMA[half]], 1)
                if stage == "T":
                    b = bank[w.phase.of[f"{a}.pT.{n}"][0]]
                    row, per = (w.a, 2 * UNITS) if half == 0 else (w.b, UNITS)
                    dve.wait_ge(ready[HIGH[half]], at(row, per, turn * UNITS + n + 1))
                    nc.vector.tensor_tensor(pT_lo[:, half, n % 2, :], b[:, :], pT_hi[:, half, n % 2, :], ALU.subtract)\
                        .then_inc(gone(w, f"{a}.pT.{n}"), 1)
                if stage == "N":
                    u = n
                    b = wait_filled(dve, w, f"{a}.pv.{u}")
                    if a == "media":
                        o = b[:, 0:4 * (width + 1)].rearrange("p (h d) -> p h d", h=4)
                    else:
                        o = sums[:, u % 2, :, 0:width + 1]
                        link(w, nc.vector.tensor_reduce(
                            o, b[:, 0:12 * (width + 1)].rearrange("p (h s d) -> p h d s", h=4, s=3), AX.X, ALU.add))
                    r = rec[:, half, u % 2, :]
                    link(w, nc.vector.reciprocal(r, o[:, :, width]))
                    num, den = o[:, :, 0:width], r.unsqueeze(2).broadcast_to([P, 4, width])
                    if a == "cross":
                        to = on_a[:, u * 4 * DC:(u + 1) * 4 * DC].rearrange("p (h d) -> p h d", h=4)
                    else:
                        num = num.rearrange("p (a b) d -> p a b d", a=2)
                        den = den.rearrange("p (a b) d -> p a b d", a=2)
                        if a == "self":
                            to = on_a[:].rearrange("p (a g e d) -> p a g e d", a=2, g=4, e=2)[:, :, u]
                        else:
                            num, den = o[:, :, 0:width], r.unsqueeze(2).broadcast_to([P, 4, width])
                            to = on_b[:].rearrange("p (a c e d) -> p a c e d", a=2, c=4, e=2)[:, u // 2, :, u % 2, :]
                    nc.vector.tensor_tensor(to, num, den, ALU.mult).then_inc(gone(w, f"{a}.pv.{u}"), 1)

            def value_parts(w, name, k, v, rest, heads):
                b = bank[w.phase.of[name][0]]
                if name[:2] == "v2":
                    dve.wait_ge(ready["v_hi_b"], at(w.b, 2, k))
                else:
                    dve.wait_ge(ready["v_hi_a"], at(w.a, 2, k))
                x = b[:, C:2 * C] if name == "ckv" else b[:, 0:H if name == "v" else 512]
                x = x.rearrange("p (h d) -> p h d", h=heads)
                ins = nc.vector.tensor_tensor(rest, x, v[:, :, 0, :], ALU.subtract)
                if name[:2] == "v2":
                    ins.then_inc(gone(w, name), 1)
                else:
                    link(w, ins)
                    link(w, nc.vector.tensor_copy(v[:, :, 1, :], rest))
                    nc.vector.tensor_tensor(v[:, :, 2, :], rest, v[:, :, 1, :], ALU.subtract).then_inc(gone(w, name), 1)

            def by_expert(w, name, x, to):
                b = wait_filled(dve, w, name)
                link(w, nc.vector.scalar_tensor_tensor(to[:], b[:, 0:H], vm[:, 0:1], x[:], ALU.mult, ALU.add))
                nc.vector.scalar_tensor_tensor(to[:], b[:, H:2 * H], vm[:, 1:2], to[:], ALU.mult, ALU.add)\
                    .then_inc(gone(w, name), 1)

            def masked_norm(w, n, x):
                dve.wait_ge(rstd_ready[n], at(w.a, 1, 1))
                for e in range(2):
                    i = nc.vector.tensor_scalar(xs[:, e, :], x[:], rstd[:, n:n + 1], vm[:, e:e + 1], ALU.mult, ALU.mult)
                i.then_inc(ready["xs"], 1)

            def statistics(w, n, x):
                link(w, nc.vector.bn_stats(bns[:], x[:]))
                dve.sem_inc(passed_dve, 1)
                nc.vector.bn_aggr(var[:, n, :], bns[:]).then_inc(var_ready[n], 1)

            def layer_norm(w, n, x):
                dve.wait_ge(rstd_ready[n], at(w.b, 1, 1))
                nc.vector.tensor_scalar(xn_b[:], x[:], var[:, n, 0:1], rstd[:, n:n + 1], ALU.subtract,
                                        ALU.mult).then_inc(ready["xn_b"], 1)

            def memory(w, m, what):
                k, src, dst, norm, out_ready = BLOCKS[m]
                if what == "mp":
                    b = wait_filled(dve, w, f"{m}.mp")
                    nc.vector.tensor_copy(mp[:], b[:, 0:H]).then_inc(gone(w, f"{m}.mp"), 1)
                if what == "s":
                    b = wait_filled(dve, w, f"{m}.score")
                    nc.vector.tensor_reduce(mmx[:, 1:2], b[:, 0:T], AX.X, ALU.max, negate=True).then_inc(ready["mneg"], 1)
                if what == "c":
                    b = wait_filled(dve, w, f"{m}.mc")
                    link(w, nc.vector.reciprocal(mmx[:, 3:4], mmx[:, 2:3]))
                    nc.vector.tensor_scalar(mc[:], b[:, 0:H], mmx[:, 3:4], None, ALU.mult)\
                        .then_inc(gone(w, f"{m}.mc"), 1)
                if what == "f":
                    wait_evacuated(dve, w, f"{m}.gate")
                    link(w, nc.vector.scalar_tensor_tensor(gth[:], gth[:], 1.0, mc[:], ALU.add, ALU.mult))
                    nc.vector.scalar_tensor_tensor(fus[:], gth[:], 0.5, src[:], ALU.mult, ALU.add)\
                        .then_inc(ready["fused"], 1)
                if what == "n":
                    if k == 1:
                        dve.wait_ge(y_stored, at(w.b, 16, 16))
                    dve.wait_ge(rstd_ready[norm], at(w.b, 1, 1))
                    nc.vector.scalar_tensor_tensor(dst[:], fus[:], rstd[:, norm:norm + 1], norm_w[:, k, :], ALU.mult,
                                                   ALU.mult).then_inc(ready[out_ready], 1)

            def step(w, name):
                what, _, n = name.partition(".")
                if w.phase is middle and name == middle.steps[0][0]:
                    assert chained[0] == LINKS_A, chained
                if w.phase is last and name == last.steps[0][0]:
                    assert chained[0] == 2 * LINKS_A + LINKS_B, chained
                    chained[0] += (B - 2) * (LINKS_A + LINKS_B)
                if what in ATT:
                    attention(w, what, n[0], int(n[1]))
                elif what in BLOCKS:
                    memory(w, what, n)
                elif name == "enc.k":
                    dve.wait_ge(ready["v_hi_a"], at(w.a, 2, 1))
                    x = bank[w.phase.of["ckv"][0]][:, 0:C].rearrange("p (u d) -> p u d", u=UNITS)
                    nc.vector.tensor_tensor(ck_parts[:, :, 1, :].bitcast(F32R), x, ck_parts[:, :, 0, :], ALU.subtract)
                    value_parts(w, "ckv", 1, v_cross[:, :, :, 0:DC], v_cross_rest[:], NH)
                elif name == "ckT":
                    b = bank[w.phase.of["ckT"][0]]
                    dve.wait_ge(ready["ckm_act"], at(w.a, 1, 1))
                    for h in range(2, 4):
                        i = nc.vector.tensor_scalar(ckm[:, :, h, :].bitcast(F32R), b[0:96, :].rearrange("p (u t) -> p u t", u=4),
                                                cst[0:96, C_M4 + h:C_M4 + h + 1], None, ALU.mult)
                    i.then_inc(gone(w, "ckT"), 1)
                elif name == "cq":
                    dve.wait_ge(ready["cq_hi"], at(w.a, 1, 1))
                    x = bank[w.phase.of["cq"][0]][:, 0:C].rearrange("p (u d) -> p u d", u=UNITS)
                    nc.vector.scalar_tensor_tensor(cq_parts[:, :, 2, :].bitcast(F32R), x, DC ** -0.5, cq_parts[:, :, 0, :],
                                                   ALU.mult, ALU.subtract).then_inc(gone(w, "cq"), 1)
                elif name == "in.n":
                    link(w, nc.vector.tensor_copy(vm[:], vm_all[:, :, bass.ds(w.a, 1)].rearrange("p e o -> p (e o)")))
                    masked_norm(w, N_IN, x_in)
                elif name == "rope.r":
                    b = wait_filled(dve, w, "qk")[:, :].rearrange("p (h s d) -> p h s d", h=2 * NH, s=2)
                    r2 = rot2[:].rearrange("p (h s d) -> p h s d", h=2 * NH, s=2)
                    nc.vector.tensor_tensor(rot[:].rearrange("p (h d) -> p h d", d=DS), b.rearrange("p h s d -> p h (s d)"),
                                            rope[:, 0:DS].unsqueeze(1).broadcast_to([P, 2 * NH, DS]), ALU.mult)
                    for s in range(2):
                        i = nc.vector.tensor_tensor(
                            r2[:, :, s, :], b[:, :, 1 - s, :],
                            rope[:, DS + 8 * s:DS + 8 * s + 8].unsqueeze(1).broadcast_to([P, 2 * NH, DS // 2]), ALU.mult)
                    i.then_inc(gone(w, "qk"), 1)
                    wait_evacuated(dve, w, "qk")
                    nc.vector.tensor_tensor(rot[:], rot[:], rot2[:], ALU.add).then_inc(ready["rot"], 1)
                    value_parts(w, "v", 2, v_self[:, :, :, 0:DS], v_self_rest[:], NH)
                elif name == "dense":
                    by_expert(w, "dense", x_in, x1)
                elif name == "ci.n":
                    dve.wait_ge(rstd_ready[N_CROSS], at(w.a, 1, 1))
                    nc.vector.tensor_scalar(xn_a[:], x1[:], rstd[:, N_CROSS:N_CROSS + 1], None, ALU.mult)\
                        .then_inc(ready["xn_a"], 1)
                elif name == "cdense":
                    b = wait_filled(dve, w, "cdense")
                    nc.vector.tensor_tensor(x2[:], b[:, 0:H], x1[:], ALU.add).then_inc(gone(w, "cdense"), 1)
                elif name == "mi.n":
                    masked_norm(w, N_ATTN, x2)
                elif what == "ffn":
                    i = int(n)
                    b = wait_filled(dve, w, name)
                    dve.wait_ge(ready["tanh"], at(w.a, FFC // 2, i + 1))
                    link(w, nc.vector.scalar_tensor_tensor(tg[:, i % 2, :], th[:, i % 2, :], 1.0, b[:, 0:2 * T], ALU.add,
                                                           ALU.mult))
                    nc.vector.scalar_tensor_tensor(hT[:, 2 * i:2 * i + 2].rearrange("p i t -> p (i t)"), tg[:, i % 2, :],
                                                   0.5, b[:, 2 * T:], ALU.mult, ALU.mult).then_inc(gone(w, name), 1)
                elif name == "down":
                    by_expert(w, "down", x2, x3)
                    if w.phase is first:
                        bias_parts()
                elif name == "encb.k":
                    dve.wait_ge(mask_loaded, at(w.b, 16, 16))
                    nc.vector.tensor_scalar(mrow[:], mm_u8[:].unsqueeze(1).broadcast_to([1, 4, T]), -NEG, NEG, ALU.mult,
                                            ALU.add).then_inc(ready["mrow"], 1)
                    for c in range(2):
                        b = wait_filled(dve, w, f"k2.{c}")
                        nc.vector.tensor_copy(kT2[:, 4 * c:4 * c + 4].rearrange("p c t -> p (c t)"), b[:, :])\
                            .then_inc(gone(w, f"k2.{c}"), 1)
                elif name == "v2":
                    for h in range(2):
                        value_parts(w, f"v2.{h}", h + 1, v_media[:, 8 * h:8 * h + 8, :, 0:DM],
                                    v_media_rest[:, 8 * h:8 * h + 8, :], 8)
                elif name == "qn.q":
                    dve.wait_ge(ready["x4"], at(w.b, 1, 1))
                    statistics(w, N_Q, x4)
                elif name == "qn.n":
                    layer_norm(w, N_Q, x4)
                elif name == "o2T.1":
                    b = wait_filled(dve, w, "o2T.1")
                    nc.vector.tensor_copy(o2T[:, 4:8, :].rearrange("p c t -> p (c t)"), b[:, :])\
                        .then_inc(gone(w, "o2T.1"), 1)
                elif name == "wo":
                    if w.phase is middle:
                        dve.wait_ge(act_setup, 1)
                    b = wait_filled(dve, w, "wo")
                    nc.vector.scalar_tensor_tensor(x5[:], b[:, 0:H], tgates[:, 0:1], x4[:], ALU.mult,
                                                   ALU.add).then_inc(gone(w, "wo"), 1)
                elif name == "hn.q":
                    wait_evacuated(dve, w, "wo")
                    statistics(w, N_FF, x5)
                elif name == "hn.n":
                    layer_norm(w, N_FF, x5)
                elif name == "w2":
                    b = wait_filled(dve, w, "w2")
                    nc.vector.scalar_tensor_tensor(x6[:], b[:, 0:H], tgates[:, 1:2], x5[:], ALU.mult,
                                                   ALU.add).then_inc(gone(w, "w2"), 1)

            run(dve, step)

        @block.tensor
        def _(pe):
            mm = nc.tensor.matmul

            pe.wait_ge(ready["onehot"], 1)
            mm(bank[5][:, 0:2 * DS], pos_f[:, 1, :], cst[:, C_COS:C_COS + 2 * DS], start=True, stop=True)\
                .then_inc(pe_setup, 1)
            pe.wait_ge(ready["masks"], 2)
            pe.wait_ge(pool_setup, POOL_SETUP)

            def need(w, phase, group, n):
                if w.phase is phase:
                    pe.wait_ge(loaded[group], 16 * n)

            def fill(w, name, *results):
                for b, n in w.drained(results, (name,)):
                    pe.wait_ge(drained[b], n)
                return bank[w.phase.of[name][0]]

            def done(w, ins, name):
                ins.then_inc(filled[w.phase.of[name][0]], 1)

            def turn(w, name, sources, *results):
                b = fill(w, name, *results)
                for k, s in enumerate(sources):
                    i = nc.tensor.transpose(b[0:s.shape[1], k * P:(k + 1) * P], s, ident)
                done(w, i, name)

            def product(w, name, width, pairs, *results, halfway=None):
                b = fill(w, name, *results)
                for k, (stationary, moving) in enumerate(pairs):
                    if halfway and k == len(pairs) // 2:
                        wait_evacuated(pe, w, halfway)
                    i = mm(b[:, 0:width], stationary, moving, start=k == 0, stop=k == len(pairs) - 1)
                done(w, i, name)

            def features(w, name, weights, xT_, outs, n_in, *results):
                b = fill(w, name, *results)
                for k, o in enumerate(outs):
                    for c in range(n_in):
                        i = mm(b[:, k * T:(k + 1) * T], weights(c, o), xT_(c), start=c == 0, stop=c == n_in - 1)
                done(w, i, name)

            def score(w, a, n):
                name = f"{a}.score.{n}"
                b = fill(w, name, *(OPERANDS[a] if n == 0 else ()))
                if a == "self":
                    r = slice(32 * n, 32 * n + 32)
                    for g in range(2):
                        mm(b[:, g * 2 * P:(g + 1) * 2 * P], qT[r, g, :], keo[r, g].rearrange("p e t -> p (e t)"),
                           start=g == 0, stop=False, skip_group_check=True)
                    i = mm(b[:, :], identb[:], causal[:].rearrange("p h k -> p (h k)"), start=False, stop=True,
                           skip_group_check=True)
                elif a == "cross":
                    i = mm(b[:, :], cqT[:, n, :].bitcast(F32R), ckm[:, n].rearrange("p h t -> p (h t)").bitcast(F32R),
                           start=True, stop=True)
                else:
                    r = slice(64 * (n % 2), 64 * (n % 2) + 64)
                    for h in range(4):
                        c = n // 2 * 4 + h
                        mm(b[:, h * P:(h + 1) * P], qT2[r, c, :], kT2[r, c, :], start=h == 0, stop=False,
                           skip_group_check=True)
                    i = mm(b[:, :], onesb[0:1, :], mrow[:].rearrange("p h t -> p (h t)"), start=False, stop=True,
                           skip_group_check=True)
                done(w, i, name)

            OPERANDS = {"self": ("v", "qkT"), "cross": ("cqT", "ckT", "ckv"), "media": ("q2.1", "k2.1")}

            def values(a, n, h):
                if a == "self":
                    return v_self[:, h // 2 * 8 + 2 * n + h % 2]
                if a == "cross":
                    return v_cross[:, 4 * n + h]
                return v_media[:, 2 * (n // 2 * 4 + h) + n % 2]

            def attention(w, a, stage, n):
                half, _, width = ATT[a]
                if stage == "S":
                    score(w, a, n)
                if stage == "T":
                    turn(w, f"{a}.pT.{n}", [pr[:, half, n % 2, h * P:(h + 1) * P] for h in range(4)], f"{a}.score.{n}")
                if stage == "V":
                    b = fill(w, f"{a}.pv.{n}", f"{a}.pT.{n}")
                    for h in range(4):
                        hi, lo = (part[:, half, n % 2, h * P:(h + 1) * P] for part in (pT_hi, pT_lo))
                        v = values(a, n, h)
                        if a == "media":
                            o = b[:, h * (width + 1):(h + 1) * (width + 1)]
                            terms = [(p_, s_) for p_ in (hi, lo) for s_ in range(3)]
                            for k, (p_, s_) in enumerate(terms):
                                i = mm(o, p_, v[:, s_, :], start=k == 0, stop=k == len(terms) - 1)
                        else:
                            o = b[:, h * 3 * (width + 1):(h + 1) * 3 * (width + 1)]
                            for k, p_ in enumerate((hi, lo)):
                                i = mm(o, p_, v.rearrange("p s d -> p (s d)"), start=k == 0, stop=k == 1)
                    done(w, i, f"{a}.pv.{n}")

            def memory(w, m, what):
                k, src, dst, norm, _ = BLOCKS[m]
                if what == "mp":
                    need(w, middle, "m", 4)
                    features(w, f"{m}.mpT", lambda c, o: w_memT[:, k, o * P:(o + 1) * P], lambda c: encbT[:], range(2), 1,
                             *(("encbT",) if m == "m0" else ()))
                    product(w, f"{m}.mp", H, [(encbT[:], w_memT[:, k, :])])
                if what == "x":
                    turn(w, f"{m}.xT", [src[:, c * P:(c + 1) * P] for c in range(2)], "w2" if m == "m1" else "m0.mp")
                if what == "s":
                    product(w, f"{m}.score", T, [(lT[:, c, :], mpT[:, c, :]) for c in range(2)], f"{m}.xT", f"{m}.mpT")
                if what == "p":
                    turn(w, f"{m}.pT", [mpr[:]], f"{m}.score")
                if what == "c":
                    product(w, f"{m}.mc", H, [(mpr_T[:], mp[:])], f"{m}.pT", f"{m}.mp")
                if what == "t":
                    turn(w, f"{m}.mcT", [mc[:, c * P:(c + 1) * P] for c in range(2)], f"{m}.mc")
                if what == "g":
                    if m == "m0":
                        if w.phase is middle:
                            pe.wait_ge(ready["bias"], 1)
                    product(w, f"{m}.gate", H, [(lT[:, c, :], w_gateT[:, k, c, :]) for c in range(4)]
                            + [(onesb[:], b_parts[:, k, :])], f"{m}.mcT")

            def step(w, name):
                what, _, n = name.partition(".")
                if what in ATT:
                    if name == "media.S0":
                        pe.wait_ge(ready["mrow"], at(w.b, 1, 1))
                        pe.wait_ge(ready["v_media"], at(w.b, 2, 2))
                    attention(w, what, n[0], int(n[1]))
                elif what in BLOCKS:
                    memory(w, what, n)
                elif name == "enc.T":
                    pe.wait_ge(enc_loaded, at(w.a, 16, 16))
                    turn(w, "encT", [enc[:]])
                elif name == "enc.k":
                    need(w, first, "ckv", 1)
                    product(w, "ckv", 2 * C, [(encT[:], w_ckv[:])], "encT")
                elif name in ("in.T", "mi.T"):
                    pe.wait_ge(ready["xs"], at(w.a, 2, 1 if what == "in" else 2))
                    turn(w, what + "T", [xs[:, e, c * P:(c + 1) * P] for c in range(2) for e in range(2)])
                elif name == "qkv":
                    need(w, first, "self", 2)
                    for part, lo, hi in (("qk", 0, 2 * H), ("v", 2 * H, 3 * H)):
                        product(w, part, hi - lo, [(xT[:, c, e, :], w_qkv[:, e, c, lo:hi]) for c in range(2) for e in range(2)],
                                "inT")
                elif name == "rope.T":
                    pe.wait_ge(ready["rot"], at(w.a, 1, 1))
                    turn(w, "qkT", [rot[:, c * P:(c + 1) * P] for c in range(4)])
                elif name == "oT":
                    turn(w, "oT", [on_a[:, c * P:(c + 1) * P] for c in range(2)], f"self.pv.{UNITS - 1}")
                elif name == "dense":
                    need(w, first, "dense", 2)
                    product(w, "dense", 2 * H, [(oT[:, c, :], w_dense[:, c, :]) for c in range(2)], "oT")
                elif name == "ci.T":
                    pe.wait_ge(ready["xn_a"], at(w.a, 1, 1))
                    turn(w, "ciT", [xn_a[:, c * P:(c + 1) * P] for c in range(2)])
                elif name == "cq":
                    need(w, first, "cross", 2)
                    product(w, "cq", C, [(nT_a[:, c, :], w_cq[:, c, :]) for c in range(2)], "ciT")
                elif name in ("ckT", "cqT"):
                    parts, source = (ck_parts, "ckv") if name == "ckT" else (cq_parts, "cq")
                    turn(w, name, [parts[:, u].rearrange("p s d -> p (s d)") for u in range(UNITS)], source)
                elif name == "coT":
                    turn(w, "coT", [on_a[:, 0:P]], f"cross.pv.{UNITS - 1}")
                elif name == "cdense":
                    product(w, "cdense", H, [(oT[:, 0, :], w_cdense[:])], "coT")
                elif what == "ffn":
                    if n == "0":
                        need(w, first, "ffn", 4)
                    b = fill(w, name, "miT")
                    for u in range(2):
                        for i in range(2):
                            at_ = b[:, (2 * u + i) * T:(2 * u + i + 1) * T]
                            for k in range(4):
                                o = 2 * int(n) + i
                                ins = mm(at_, w_gu[:, k % 2, k // 2, u, o * P:(o + 1) * P], xT[:, k // 2, k % 2, :],
                                         start=k == 0, stop=k == 3)
                    done(w, ins, name)
                elif name == "down":
                    need(w, first, "down", 4)
                    b = fill(w, name, "ffn.0")
                    for i in range(FFC):
                        if i in (2, 4):
                            wait_evacuated(pe, w, f"ffn.{i // 2}")
                        ins = mm(b[:, :], hT[:, i, :], w_down[:, i, :], start=i == 0, stop=i == FFC - 1)
                    done(w, ins, name)
                elif name == "encb.T":
                    pe.wait_ge(encb_loaded, at(w.b, 16, 16))
                    turn(w, "encbT", [encb[:]])
                elif name == "encb.k":
                    need(w, middle, "kv2", 1)
                    for c in range(2):
                        features(w, f"k2.{c}", lambda _, o: w_kv2[:, o * P:(o + 1) * P], lambda _: encbT[:],
                                 range(4 * c, 4 * c + 4), 1, "encbT")
                elif name == "v2":
                    for h in range(2):
                        product(w, f"v2.{h}", 512, [(encbT[:], w_kv2[:, INNER + h * 512:INNER + (h + 1) * 512])])
                elif name in ("qn.T", "hn.T"):
                    pe.wait_ge(ready["xn_b"], at(w.b, 2, 1 if what == "qn" else 2))
                    turn(w, what + "T", [xn_b[:, c * P:(c + 1) * P] for c in range(2)])
                elif what in ("q2", "ff2"):
                    need(w, middle, what, 1 if what == "q2" else 2)
                    wt = w_q2 if what == "q2" else w_1
                    features(w, name, lambda c, o: wt[:, c, o * P:(o + 1) * P], lambda c: nT_b[:, c, :],
                             range(4 * int(n), 4 * int(n) + 4), 2, "qnT" if what == "q2" else "hnT")
                elif what == "o2T":
                    h = int(n)
                    turn(w, name, [on_b[:, c * P:(c + 1) * P] for c in range(4 * h, 4 * h + 4)], f"media.pv.{2 * h + 1}")
                elif name == "wo":
                    need(w, middle, "o2", 1)
                    product(w, "wo", H, [(o2T[:, c, :], w_o2[:, c, :]) for c in range(MC)], "o2T.0", halfway="o2T.1")
                elif name == "w2":
                    product(w, "w2", H, [(h2T[:, c, :], w_2[:, c, :]) for c in range(MC)], "ff2.0", halfway="ff2.1")

            run(pe, step)


INS = ["x", "ctx_1024", "pos_1xS", "mask_BxS_ik0", "mask_BxS2_bk0"]
WEIGHTS = {
    0: ["ln_in_w", "ln_post_attn_w", "ln_post_cross_w", "v_qkv", "l_qkv", "v_dense", "l_dense", "cq_w", "ckv_w",
        "cdense_w", "v_gate", "v_up", "v_down", "l_gate", "l_up", "l_down"],
    1: ["W_mem", "W_gate", "b_gate", "norm_w"],
    2: ["ln_q_g", "ln_q_b", "Wq", "Wkv", "Wo", "attn_gate", "ln_ff_g", "ln_ff_b", "W1", "W2", "ff_gate"],
    3: ["W_mem", "W_gate", "b_gate", "norm_w"],
}


def kernel(**inputs):
    import concourse.bacc as bacc
    from concourse.bass_utils import run_bass_kernel_spmd

    nc = bacc.Bacc("TRN2", target_bir_lowering=False, num_devices=1)
    arrays, args = {}, {}
    given = {n: np.ascontiguousarray(inputs[n]) for n in INS}
    for b, names in WEIGHTS.items():
        for n in names:
            given[f"L{b}_xattn_{n}"] = np.ascontiguousarray(inputs[f"L{b}_xattn_{n}"])
    given["constants"] = constants()
    given["types_T"] = np.ascontiguousarray(given.pop("mask_BxS_ik0").T)
    given["columns"] = np.ascontiguousarray(np.concatenate(
        [given.pop(n).reshape(2, P).T for n in (
            "L0_xattn_ln_in_w", "L0_xattn_ln_post_cross_w", "L0_xattn_ln_post_attn_w", "L2_xattn_ln_q_g",
            "L2_xattn_ln_q_b", "L2_xattn_ln_ff_g", "L2_xattn_ln_ff_b")], axis=1))
    for n in ("L1_xattn_W_mem", "L1_xattn_W_gate", "L3_xattn_W_mem", "L3_xattn_W_gate"):
        given[n] = np.ascontiguousarray(given[n].T)
    for name, a in given.items():
        arrays[f"in_{name}"] = a
        dtype = U8 if a.dtype == bool else mybir.dt.from_np(a.dtype)
        args[name] = nc.dram_tensor(f"in_{name}", a.shape, dtype, kind="ExternalInput").ap()
    out = nc.dram_tensor("out", (B, T, H), F32, kind="ExternalOutput").ap()
    build(nc, args, out)
    r = run_bass_kernel_spmd(nc, [arrays], core_ids=[0])
    return r.results[0]["out"]
```
